# Optimizing a Trainium2 kernel written in Bass

```python
import numpy as np
import jax
import jax.numpy as jnp

def _softmax(x, axis=-1):
    return jax.nn.softmax(x, axis=axis)

def _gelu(x):
    return jax.nn.gelu(x, approximate=True)

def _silu(x):
    return jax.nn.silu(x)

def _sigmoid(x):
    return jax.nn.sigmoid(x)

def _layernorm(x, axis=-1, eps=1e-05):
    m = jnp.mean(x, axis=axis, keepdims=True)
    v = jnp.var(x, axis=axis, keepdims=True)
    return (x - m) / jnp.sqrt(v + eps)

def _scatter_add(tgt, idx, src, axis=0):
    return tgt.at[idx].add(src)

def _segment_sum(src, seg, n):
    return jax.ops.segment_sum(src, seg, n)
kernel_name = 'mk_decoder_preln_d1_seqx_r4_f8b758'

def setup_inputs(seed: int=0):
    np.random.seed(seed)
    _w = jnp.asarray

    def _rec_inputs():
        import jax
        import jax.numpy as jnp
        _rk = jax.random.key(seed)
        x = -0.0002928 + 1 * jax.random.normal(jax.random.fold_in(_rk, 1), (16, 128, 256), jnp.float32)
        _lenS = 128 - jax.random.randint(jax.random.fold_in(_rk, 7), (16,), 0, max(1, 128 // 4) + 1, jnp.int32)
        _lenS2 = 128 - jax.random.randint(jax.random.fold_in(_rk, 8), (16,), 0, max(1, 128 // 4) + 1, jnp.int32)
        _ctx_512P = jax.random.normal(jax.random.fold_in(_rk, 11), (16, 16, 128), jnp.float32)
        _ctx_512c = jax.random.dirichlet(jax.random.fold_in(_rk, 511), 0.3 * jnp.ones((16,), jnp.float32), (16, 128))
        _ctx_512t = jnp.einsum('bsk,bkd->bsd', _ctx_512c, _ctx_512P)
        _ctx_512t = _ctx_512t * jax.lax.rsqrt(jnp.mean(jnp.square(_ctx_512t)) + 1e-12) * 0.953939
        ctx_512 = -1.52775e-05 + 0.999936 * (_ctx_512t + 0.3 * jax.random.normal(jax.random.fold_in(_rk, 611), (16, 128, 128), jnp.float32))
        return (x, ctx_512)
    x, ctx_512 = _rec_inputs()

    def _L0_attn_setup():
        import jax, jax.numpy as jnp
        import numpy as np
        CLIP_VAL = 8
        FRACTION_BITS = 12
        SCALE = float(2 ** FRACTION_BITS)
        EPS = 1.0 / SCALE
        HEADS = 16
        DIM_HEAD = 64

        def make_fxp(x):
            c = CLIP_VAL - EPS
            x = jnp.clip(x, -c, c)
            return jnp.trunc(x * SCALE) / SCALE
        key = jax.random.key(seed)
        k1, k2, k3, k4 = jax.random.split(key, 4)
        B, N, D = (4, 512, 256)
        inner = HEADS * DIM_HEAD
        x = jax.random.normal(k1, (B, N, D), dtype=jnp.float32)
        w_qkv = jax.random.normal(k2, (3 * inner, D), dtype=jnp.float32) * D ** (-0.5)
        w_proj = jax.random.normal(k3, (D, inner), dtype=jnp.float32) * inner ** (-0.5)
        b_proj = jax.random.normal(k4, (D,), dtype=jnp.float32) * 0.01
        return {'x': x, 'w_qkv': w_qkv, 'w_proj': w_proj, 'b_proj': b_proj}
    _L0_attn_all = _L0_attn_setup()
    _L0_attn_in = {k: v for k, v in _L0_attn_all.items() if k in ('w_qkv', 'w_proj', 'b_proj')}
    del _L0_attn_all

    def _L0_xattn_setup():
        import jax, jax.numpy as jnp
        import numpy as np
        NUM_HEADS = 16
        HEAD_DIM = 64
        Q_DIM = 256
        KV_DIM = 128
        INNER = NUM_HEADS * HEAD_DIM
        key = jax.random.key(seed)
        ks = jax.random.split(key, 7)
        B, N, M = (32, 128, 512)
        q = jax.random.normal(ks[0], (B, N, Q_DIM), dtype=jnp.float32)
        kv = jax.random.normal(ks[1], (B, M, KV_DIM), dtype=jnp.float32)
        Wq = jax.random.normal(ks[2], (Q_DIM, INNER), dtype=jnp.float32) / np.sqrt(Q_DIM)
        Wk = jax.random.normal(ks[3], (KV_DIM, INNER), dtype=jnp.float32) / np.sqrt(KV_DIM)
        Wv = jax.random.normal(ks[4], (KV_DIM, INNER), dtype=jnp.float32) / np.sqrt(KV_DIM)
        Wo = jax.random.normal(ks[5], (INNER, Q_DIM), dtype=jnp.float32) / np.sqrt(INNER)
        bo = jax.random.normal(ks[6], (Q_DIM,), dtype=jnp.float32) * 0.01
        return {'q': q, 'kv': kv, 'Wq': Wq, 'Wk': Wk, 'Wv': Wv, 'Wo': Wo, 'bo': bo}
    _L0_xattn_all = _L0_xattn_setup()
    _L0_xattn_in = {k: v for k, v in _L0_xattn_all.items() if k in ('Wq', 'Wk', 'Wv', 'Wo', 'bo')}
    del _L0_xattn_all

    def _L0_ffn_setup():
        import jax, jax.numpy as jnp
        import numpy as np
        D_MODEL, D_FF, NUM_EXPERTS, RANK, TOP_K = (256, 1024, 8, 16, 2)
        B, S = (8, 512)

        def _expert_ffn(h, wi_w, wo_w, A, Bm):
            inter = jnp.einsum('bsd,fd->bsf', h, wi_w)
            lora = jnp.einsum('bsr,fr->bsf', jnp.einsum('bsd,rd->bsr', h, A), Bm)
            inter = jax.nn.relu(inter + lora)
            return jnp.einsum('bsf,df->bsd', inter, wo_w)
        key = jax.random.key(seed)
        ks = jax.random.split(key, 8)
        hidden_states = jax.random.normal(ks[0], (B, S, D_MODEL), dtype=jnp.float32)
        wi_w = jax.random.normal(ks[1], (D_FF, D_MODEL), dtype=jnp.float32) * (1.0 / np.sqrt(D_MODEL))
        wo_w = jax.random.normal(ks[2], (D_MODEL, D_FF), dtype=jnp.float32) * (1.0 / np.sqrt(D_FF))
        lora_As = jax.random.uniform(ks[3], (NUM_EXPERTS, RANK, D_MODEL), dtype=jnp.float32, minval=-1.0, maxval=1.0) / np.sqrt(D_MODEL)
        lora_Bs = jax.random.normal(ks[4], (NUM_EXPERTS, D_FF, RANK), dtype=jnp.float32) * 0.02
        top_k_indices = jnp.arange(TOP_K, dtype=jnp.int32)
        top_k_values = jax.random.uniform(ks[5], (TOP_K,), dtype=jnp.float32)
        return {'hidden_states': hidden_states, 'wi_w': wi_w, 'wo_w': wo_w, 'lora_As': lora_As, 'lora_Bs': lora_Bs, 'top_k_indices': top_k_indices, 'top_k_values': top_k_values}
    _L0_ffn_all = _L0_ffn_setup()
    _L0_ffn_in = {k: v for k, v in _L0_ffn_all.items() if k in ('wi_w', 'wo_w', 'lora_As', 'lora_Bs', 'top_k_indices', 'top_k_values')}
    del _L0_ffn_all
    return {'x': x, 'ctx_512': ctx_512, 'L0_attn_w_qkv': _L0_attn_in['w_qkv'], 'L0_attn_w_proj': _L0_attn_in['w_proj'], 'L0_attn_b_proj': _L0_attn_in['b_proj'], 'L0_xattn_Wq': _L0_xattn_in['Wq'], 'L0_xattn_Wk': _L0_xattn_in['Wk'], 'L0_xattn_Wv': _L0_xattn_in['Wv'], 'L0_xattn_Wo': _L0_xattn_in['Wo'], 'L0_xattn_bo': _L0_xattn_in['bo'], 'L0_ffn_wi_w': _L0_ffn_in['wi_w'], 'L0_ffn_wo_w': _L0_ffn_in['wo_w'], 'L0_ffn_lora_As': _L0_ffn_in['lora_As'], 'L0_ffn_lora_Bs': _L0_ffn_in['lora_Bs'], 'L0_ffn_top_k_indices': _L0_ffn_in['top_k_indices'], 'L0_ffn_top_k_values': _L0_ffn_in['top_k_values']}

def reference(x, ctx_512, L0_attn_w_qkv, L0_attn_w_proj, L0_attn_b_proj, L0_xattn_Wq, L0_xattn_Wk, L0_xattn_Wv, L0_xattn_Wo, L0_xattn_bo, L0_ffn_wi_w, L0_ffn_wo_w, L0_ffn_lora_As, L0_ffn_lora_Bs, L0_ffn_top_k_indices, L0_ffn_top_k_values):
    import jax
    import jax.numpy as jnp

    def _L0_attn_ref(x, w_qkv, w_proj, b_proj):
        import jax, jax.numpy as jnp
        import numpy as np
        CLIP_VAL = 8
        FRACTION_BITS = 12
        SCALE = float(2 ** FRACTION_BITS)
        EPS = 1.0 / SCALE
        HEADS = 16
        DIM_HEAD = 64

        def make_fxp(x):
            c = CLIP_VAL - EPS
            x = jnp.clip(x, -c, c)
            return jnp.trunc(x * SCALE) / SCALE
        B, N, D = x.shape
        h, d = (HEADS, DIM_HEAD)
        scale = d ** (-0.5)
        qkv = jnp.einsum('bnd,ed->bne', x, w_qkv)
        q, k, v = jnp.split(qkv, 3, axis=-1)
        tohd = lambda t: t.reshape(B, N, h, d).transpose(0, 2, 1, 3)
        q, k, v = (make_fxp(tohd(q)), make_fxp(tohd(k)), make_fxp(tohd(v)))
        dots = make_fxp(jnp.einsum('bhnd,bhmd->bhnm', q, k) * scale)
        attn = make_fxp(jax.nn.softmax(dots, axis=-1))
        attn = make_fxp(attn)
        out = make_fxp(jnp.einsum('bhnm,bhmd->bhnd', attn, v))
        out = out.transpose(0, 2, 1, 3).reshape(B, N, h * d)
        out = make_fxp(jnp.einsum('bne,de->bnd', out, w_proj) + b_proj)
        out = make_fxp(out)
        return out

    def _L0_xattn_ref(q, kv, Wq, Wk, Wv, Wo, bo):
        import jax, jax.numpy as jnp
        import numpy as np
        NUM_HEADS = 16
        HEAD_DIM = 64
        Q_DIM = 256
        KV_DIM = 128
        INNER = NUM_HEADS * HEAD_DIM
        B, N, _ = q.shape
        M = kv.shape[1]
        scale = HEAD_DIM ** (-0.5)
        qh = (q @ Wq).reshape(B, N, NUM_HEADS, HEAD_DIM).transpose(0, 2, 1, 3)
        kh = (kv @ Wk).reshape(B, M, NUM_HEADS, HEAD_DIM).transpose(0, 2, 1, 3)
        vh = (kv @ Wv).reshape(B, M, NUM_HEADS, HEAD_DIM).transpose(0, 2, 1, 3)
        scores = jnp.einsum('bhnd,bhmd->bhnm', qh, kh) * scale
        attn = jax.nn.softmax(scores, axis=-1)
        out = jnp.einsum('bhnm,bhmd->bhnd', attn, vh)
        out = out.transpose(0, 2, 1, 3).reshape(B, N, INNER)
        return out @ Wo + bo

    def _L0_ffn_ref(hidden_states, wi_w, wo_w, lora_As, lora_Bs, top_k_indices, top_k_values):
        import jax, jax.numpy as jnp
        import numpy as np
        D_MODEL, D_FF, NUM_EXPERTS, RANK, TOP_K = (256, 1024, 8, 16, 2)
        B, S = (8, 512)

        def _expert_ffn(h, wi_w, wo_w, A, Bm):
            inter = jnp.einsum('bsd,fd->bsf', h, wi_w)
            lora = jnp.einsum('bsr,fr->bsf', jnp.einsum('bsd,rd->bsr', h, A), Bm)
            inter = jax.nn.relu(inter + lora)
            return jnp.einsum('bsf,df->bsd', inter, wo_w)
        out = jnp.zeros_like(hidden_states)
        for k in range(top_k_values.shape[0]):
            A = jnp.take(lora_As, top_k_indices[k], axis=0)
            Bm = jnp.take(lora_Bs, top_k_indices[k], axis=0)
            out = out + top_k_values[k] * _expert_ffn(hidden_states, wi_w, wo_w, A, Bm)
        return out
    x = x + _L0_attn_ref(_layernorm(x, axis=-1), L0_attn_w_qkv, L0_attn_w_proj, L0_attn_b_proj)
    x = x + _L0_xattn_ref(_layernorm(x, axis=-1), ctx_512, L0_xattn_Wq, L0_xattn_Wk, L0_xattn_Wv, L0_xattn_Wo, L0_xattn_bo)
    x = x + _L0_ffn_ref(_layernorm(x, axis=-1), L0_ffn_wi_w, L0_ffn_wo_w, L0_ffn_lora_As, L0_ffn_lora_Bs, L0_ffn_top_k_indices, L0_ffn_top_k_values)
    return x

_drawn_inputs = setup_inputs


def setup_inputs(seed=0):
    import zlib

    import numpy as np

    out = dict(_drawn_inputs(seed))
    spreads = {}
    factors = {'L0_attn_b_proj': 7.223,
     'L0_xattn_bo': 6.913,
     'L0_ffn_lora_As': 2.825,
     'L0_ffn_lora_Bs': 2.81,
     'L0_ffn_top_k_values': 8.0}
    for name, (base, spread) in spreads.items():
        noise = np.random.default_rng([zlib.crc32(name.encode()), seed]).standard_normal(out[name].shape)
        drawn = base * np.exp(spread * noise) if base else spread * noise
        out[name] = jnp.asarray(drawn.astype(out[name].dtype))
    for name, factor in factors.items():
        out[name] = (out[name] * factor).astype(out[name].dtype)
    return out
```

```python
import numpy as np
import concourse.bass as bass
from concourse import mybir
from concourse.alu_op_type import AluOpType as ALU

F32 = mybir.dt.float32
F32R = mybir.dt.float32r
BF16 = mybir.dt.bfloat16
I16 = mybir.dt.int16
I32 = mybir.dt.int32
ACT = mybir.ActivationFunctionType
AX = mybir.AxisListType.X

P = 128
B, NT, D = 16, 128, 256
H, DH = 16, 64
E = H * DH
F = 1024
CTX = 128
RANK = 16
GB = 4
G = B // GB
TOK = GB * NT
KD = D // P
NP = H // 2
NF = F // P
FIX = 4096.0
GROW = 1.0 + 2.0 ** -22
LOW = -(8.0 * FIX - 1.0)
EPS = 1e-5


def sbuf_map(nc):
    state = {"at": (nc.sbuf_base + 63) // 64 * 64}

    def place(name, shape, dtype, at=None):
        nbytes = int(np.prod(shape[1:])) * mybir.dt.size(dtype)
        nbytes = (nbytes + 31) // 32 * 32
        if at is None:
            at = state["at"]
            state["at"] = at + nbytes
        return nc.alloc_sbuf_tensor_at(name, list(shape), dtype, offset=at), at, at + nbytes

    return place, state


def block_index(s):
    return 4 * s if s < 4 else 16 + 2 * (s - 4)


BLOCKS = block_index(8)


def build(nc, x, ctx, w_qkv, w_proj, b_proj, Wq, Wk, Wv, Wo, bo, wi_w, wo_w, lora_As, lora_Bs,
          top_i, top_v, out):
    place, mem = sbuf_map(nc)

    def sb(name, shape, dtype, at=None):
        return place(name, shape, dtype, at)[0]

    x_sb = sb("x_sb", [P, B, D], F32)
    region_a = mem["at"]
    wqkvT_hi = sb("wqkvT_hi", [P, KD, 3 * E], F32R)
    wqkvT_lo = sb("wqkvT_lo", [P, KD, 3 * E], F32R)
    wpT_hi = sb("wpT_hi", [P, NP, D], F32R)
    wpT_lo = sb("wpT_lo", [P, NP, D], F32R)
    region_b = mem["at"]
    wq_hi = sb("wq_hi", [P, KD, E], F32R)
    wq_lo = sb("wq_lo", [P, KD, E], F32R)
    wk_hi = sb("wk_hi", [P, E], F32R)
    wk_lo = sb("wk_lo", [P, E], F32R)
    wv_hi = sb("wv_hi", [P, E], F32R)
    wv_lo = sb("wv_lo", [P, E], F32R)
    wo_hi = sb("wo_hi", [P, NP, D], F32R)
    wo_lo = sb("wo_lo", [P, NP, D], F32R)
    wqkv_raw, _, nxt = place("wqkv_raw", [P, 3 * NP, D], F32, at=region_b)
    wp_raw, _, nxt = place("wp_raw", [P, KD, E], F32, at=nxt)
    raw_b = sb("raw_b", [P, E], F32)
    xn = sb("xn", [P, GB, D], F32)
    xnT_hi = sb("xnT_hi", [P, KD, TOK], F32R)
    xnT_lo = sb("xnT_lo", [P, KD, TOK], F32R)
    v_sb = sb("v_sb", [P, GB, E], F32)
    q_sb = sb("q_sb", [P, 2, TOK], F32)
    k_sb = sb("k_sb", [P, 2, TOK], F32)
    e_sb = sb("e_sb", [P, 8, NT], F32)
    p_int = sb("p_int", [P, 8, NT], I16)
    y_sb = sb("y_sb", [P, 2, TOK], F32)
    aT_sb = sb("aT_sb", [P, 8, NT], F32)
    oT_hi = sb("oT_hi", [P, TOK], F32R)
    oT_lo = sb("oT_lo", [P, TOK], F32R)
    sgn = sb("sgn", [P, 2, TOK], BF16)
    ri = sb("ri", [P, 2, TOK], I16)
    near0 = sb("near0", [P, 2, TOK], F32)
    si = sb("si", [P, 2, TOK], I16)
    oi = sb("oi", [P, TOK], I16)
    ident = sb("ident", [P, P], F32)
    ident_b = sb("ident_b", [P, P], BF16)
    bias_a = sb("bias_a", [P, D], F32)
    bn_st = sb("bn_st", [P, GB, 6], F32)
    mv = sb("mv", [P, GB, 2], F32)
    veps = sb("veps", [P, GB], F32)
    rstd = sb("rstd", [P, GB], F32)
    mhalf = sb("mhalf", [P, GB], F32)
    sums = sb("sums", [P, 8], F32)
    rsum = sb("rsum", [P, 8], F32)
    rsc = sb("rsc", [P, 8], F32)
    mx = sb("mx", [P, 8], F32)
    neg_max = sb("neg_max", [P, 8], F32)
    bias_b = sb("bias_b", [P, D], F32)
    growth = sb("growth", [P, 8], F32)
    top_sb = sb("top_sb", [P, 2], F32)

    ctx_sb, _, nxt = place("ctx_sb", [P, GB, CTX], F32, at=region_a)
    cT_hi, _, nxt = place("cT_hi", [P, TOK], F32R, at=nxt)
    cT_lo, _, nxt = place("cT_lo", [P, TOK], F32R, at=nxt)
    p_f, _, nxt = place("p_f", [P, 8, NT], F32, at=nxt)
    wi_raw, _, nxt = place("wi_raw", [P, NF, D], F32, at=nxt)
    wd_raw, _, nxt = place("wd_raw", [P, KD, F], F32, at=nxt)
    lb_raw, _, nxt = place("lb_raw", [P, NF, 2, RANK], F32, at=nxt)
    lb1, _, nxt = place("lb1", [P, NF, 3, 2, RANK], F32, at=nxt)
    lb2, _, nxt = place("lb2", [P, NF, 3, 2, RANK], F32, at=nxt)
    la_raw, _, nxt = place("la_raw", [2 * RANK, D], F32, at=nxt)
    idx_sb, _, nxt = place("idx_sb", [1, 2], I32, at=nxt)
    hid0, _, nxt = place("hid0", [P, 2, TOK], F32, at=nxt)
    relu1, _, nxt = place("relu1", [P, TOK], F32, at=nxt)
    hid, _, nxt = place("hid", [P, TOK], F32, at=nxt)
    lowT, _, nxt = place("lowT", [96, TOK], F32R, at=nxt)
    assert nxt <= region_b
    wiT_hi, _, nxt = place("wiT_hi", [P, KD, F], F32R, at=region_b)
    wiT_lo, _, nxt = place("wiT_lo", [P, KD, F], F32R, at=nxt)
    wdT_hi, _, nxt = place("wdT_hi", [P, NF, D], F32R, at=nxt)
    wdT_lo, _, nxt = place("wdT_lo", [P, NF, D], F32R, at=nxt)
    lb1T, _, nxt = place("lb1T", [96, F], F32R, at=nxt)
    lb2T, _, nxt = place("lb2T", [96, F], F32R, at=nxt)
    laT_hi, _, nxt = place("laT_hi", [P, KD, P], F32R, at=nxt)
    laT_lo, _, nxt = place("laT_lo", [P, KD, P], F32R, at=nxt)
    assert mem["at"] <= nc.sbuf_usable_end, mem["at"] - nc.sbuf_usable_end

    banks = [nc.alloc_psum_tensor(f"bank{i}", [P, 512], F32) for i in range(8)]
    y_ps = banks[0:2]
    proj_ps = banks[2:4]
    s_ps = banks[4:6]
    t_ps = banks[6]
    o_ps = banks[7]
    one_ps = banks[2]
    pT_ps = (banks[3], banks[6])
    low_ps = banks[2]
    up_ps = banks[4:8]

    names = []

    def sem(name):
        names.append(name)
        return nc.alloc_semaphore(name)

    ld_x0, ld_xr, ld_wq, ld_wk, ld_wv, ld_wp, ld_b = (
        sem(n) for n in ("ld_x0", "ld_xr", "ld_wq", "ld_wk", "ld_wv", "ld_wp", "ld_b"))
    out_done = sem("out_done")
    ld_raw, ld_bhi, ld_bb = sem("ld_raw"), sem("ld_bhi"), sem("ld_bb")
    ld_ctx, ld_cw, ld_idx, ld_top = sem("ld_ctx"), sem("ld_cw"), sem("ld_idx"), sem("ld_top")
    wb_lo, g_tick = sem("wb_lo"), sem("g_tick")
    b_cT, b_chi, b_clo, b_blk, b_q, b_k, b_v = (
        sem(n) for n in ("b_cT", "b_chi", "b_clo", "b_blk", "b_q", "b_k", "b_v"))
    b_S, b_mx, b_nm, b_e, b_rs, b_p, b_T = (sem(n) for n in ("b_S", "b_mx", "b_nm", "b_e", "b_rs", "b_p", "b_T"))
    b_pT, b_av, b_ohi, b_olo, b_pj = (sem(n) for n in ("b_pT", "b_av", "b_ohi", "b_olo", "b_pj"))
    b_z, b_x = sem("b_z"), sem("b_x")
    g_lb, cw_T, cw_hi, cw_lo = sem("g_lb"), sem("cw_T"), sem("cw_hi"), sem("cw_lo")
    c_t, c_thi, c_tlo, c_u, c_u2 = (sem(n) for n in ("c_t", "c_thi", "c_tlo", "c_u", "c_u2"))
    c_g0, c_r1, c_g, c_ghi, c_glo, c_dn, c_x = (sem(n) for n in ("c_g0", "c_r1", "c_g", "c_ghi", "c_glo", "c_dn", "c_x"))
    g_const, g_rstd = sem("g_const"), sem("g_rstd")
    w_T, w_hi, w_lo = sem("w_T"), sem("w_hi"), sem("w_lo")
    idb = sem("idb")
    ln_bn, ln_mv, ln_xn, ln_T, ln_hi, ln_lo = (sem(n) for n in ("ln_bn", "ln_mv", "ln_xn", "ln_T", "ln_hi", "ln_lo"))
    g_veps = sem("g_veps")
    a_blk, a_sgn, a_ri, a_fx = sem("a_blk"), sem("a_sgn"), sem("a_ri"), sem("a_fx")
    a_S, a_y, a_near, a_si, a_clip, a_e = (sem(n) for n in ("a_S", "a_y", "a_near", "a_si", "a_clip", "a_e"))
    a_rs, a_rsc, a_p, a_T, a_aT = (sem(n) for n in ("a_rs", "a_rsc", "a_p", "a_T", "a_aT"))
    a_av, a_onear, a_oi, a_ohi, a_olo, a_pj = (sem(n) for n in ("a_av", "a_onear", "a_oi", "a_ohi", "a_olo", "a_pj"))
    a_z, a_zn, a_zi, a_zf, a_x = (sem(n) for n in ("a_z", "a_zn", "a_zi", "a_zf", "a_x"))

    def wait(eng, s, value):
        if isinstance(value, int) and value <= 0:
            return
        eng.wait_ge(s, value)

    PREP = []
    for sec in range(3):
        for half in range(2):
            for kt in range(KD):
                PREP.append(("qkv", sec * 8 + half * 4, kt))
    for et in range(0, NP, 2):
        PREP.append(("proj", et, None))

    B_CHUNKS = [(Wq.rearrange("(t p) e -> p t e", p=P)[:, i, :], wq_hi[:, i, :], wq_lo[:, i, :]) for i in range(KD)]
    B_CHUNKS += [(Wk, wk_hi[:, :], wk_lo[:, :]), (Wv, wv_hi[:, :], wv_lo[:, :])]
    B_CHUNKS += [(Wo.rearrange("(t p) d -> p t d", p=P)[:, 4 * i:4 * i + 4, :], wo_hi[:, 4 * i:4 * i + 4, :],
                  wo_lo[:, 4 * i:4 * i + 4, :]) for i in range(2)]

    C_PREP = [("up", t, kt) for t in (0, 4) for kt in range(KD)] + [("down", t, None) for t in range(0, NF, 2)]
    C_PREP += [("lb1", t, None) for t in (0, 4)] + [("lb2", t, None) for t in (0, 4)] + [("la", 0, None)]

    with nc.Block() as block:

        @block.sync
        def _(sp):
            sp.dma_start(x_sb[:, 0:GB, :], x[0:GB].rearrange("b p d -> p b d")).then_inc(ld_x0, 16)
            rows = w_qkv.rearrange("(t p) d -> p t d", p=P)
            for i, s_ in enumerate((ld_wq, ld_wk, ld_wv)):
                sp.dma_start(wqkv_raw[:, 8 * i:8 * i + 8, :], rows[:, 8 * i:8 * i + 8, :]).then_inc(s_, 16)
            sp.dma_start(wp_raw[:, :, :], w_proj.rearrange("(t p) e -> p t e", p=P)).then_inc(ld_wp, 16)
            for g in range(1, G):
                sp.dma_start(x_sb[:, g * GB:(g + 1) * GB, :],
                             x[g * GB:(g + 1) * GB].rearrange("b p d -> p b d")).then_inc(ld_xr, 16)
            sp.dma_start(bias_a[:, :], b_proj.partition_broadcast(P)).then_inc(ld_b, 16)
            sp.dma_start(bias_b[:, :], bo.partition_broadcast(P)).then_inc(ld_bb, 16)
            sp.dma_start(top_sb[:, :], top_v.partition_broadcast(P)).then_inc(ld_top, 16)
            sp.wait_ge(w_lo, len(PREP))
            for n, (src, hi, lo) in enumerate(B_CHUNKS):
                wait(sp, wb_lo, n)
                dst = raw_b[:, :] if len(src.shape) == 2 else raw_b[:, :].rearrange("p (a d) -> p a d", d=src.shape[2])
                sp.dma_start(dst, src).then_inc(ld_raw, 16)
            sp.wait_ge(a_pj, NP * G)
            sp.dma_start(idx_sb[:, :], top_i.rearrange("(a k) -> a k", a=1)).then_inc(ld_idx, 16)
            for g in range(G):
                wait(sp, b_cT, g)
                sp.dma_start(ctx_sb[:, :, :], ctx[g * GB:(g + 1) * GB].rearrange("b p d -> p b d")).then_inc(ld_ctx, 16)
                if g == 0:
                    sp.dma_start(wi_raw[:, :, :], wi_w.rearrange("(t p) d -> p t d", p=P)).then_inc(ld_cw, 16)
                    sp.dma_start(wd_raw[:, :, :], wo_w.rearrange("(t p) f -> p t f", p=P)).then_inc(ld_cw, 16)
                    sp.wait_ge(ld_idx, 16)
                    for k in range(2):
                        expert = sp.value_load(idx_sb[0:1, k:k + 1], min_val=0, max_val=lora_As.shape[0] - 1)
                        sp.dma_start(la_raw[k * RANK:(k + 1) * RANK, :],
                                     lora_As[bass.ds(expert, 1), :, :].rearrange("a r d -> (a r) d")).then_inc(ld_cw, 16)
                        sp.dma_start(lb_raw[:, :, k, :],
                                     lora_Bs[bass.ds(expert, 1), :, :].rearrange("a (t p) r -> p (a t) r", p=P)).then_inc(ld_cw, 16)
            for g in range(G):
                sp.wait_ge(c_x, 2 * g + 2)
                sp.dma_start(out[g * GB:(g + 1) * GB].rearrange("b p d -> p b d"),
                             x_sb[:, g * GB:(g + 1) * GB, :]).then_inc(out_done, 16)
            sp.wait_ge(out_done, 16 * G)

        @block.gpsimd
        def _(pool):
            nc.gpsimd.memset(ident[:, :], 0.0).then_inc(g_const, 1)
            nc.gpsimd.memset(mhalf[:, :], -0.5).then_inc(g_const, 1)
            nc.gpsimd.memset(growth[:, :], FIX * GROW).then_inc(g_const, 1)
            pool.wait_ge(g_const, 3)
            nc.gpsimd.affine_select(out=ident[:, :], in_=ident[:, :], compare_op=ALU.not_equal, fill=1.0,
                                    base=0, pattern=[[-1, P]], channel_multiplier=1).then_inc(g_const, 1)

            def inv_std(n):
                wait(pool, ln_mv, n + 1)
                nc.gpsimd.sem_inc(g_tick, 1)
                nc.gpsimd.tensor_scalar(veps[:, :], mv[:, :, 1], EPS, None, ALU.add).then_inc(g_veps, 1)
                wait(pool, g_veps, n + 1)
                nc.gpsimd.tensor_tensor(rstd[:, :], veps[:, :], mhalf[:, :], ALU.pow).then_inc(g_rstd, 1)

            def a_weights(n):
                wait(pool, a_rs, n + 1)
                nc.gpsimd.tensor_tensor(rsc[:, :], rsum[:, :], growth[:, :], ALU.mult).then_inc(a_rsc, 1)
                wait(pool, a_T, n)
                wait(pool, a_rsc, n + 1)
                nc.gpsimd.sem_inc(g_tick, 1)
                for t in range(8):
                    i = nc.gpsimd.tensor_scalar(p_int[:, t, :], e_sb[:, t, :], rsc[:, t:t + 1], -0.5,
                                                ALU.mult, ALU.add)
                i.then_inc(a_p, 1)

            def a_slot(g, s, first=False):
                if not (first and s == 0):
                    a_weights(NP * g + s - 1)
                if s == 4:
                    inv_std(g + 1)

            inv_std(0)
            pool.wait_ge(w_lo, len(PREP))
            for src, hi, lo in B_CHUNKS:
                nc.gpsimd.dma_start(hi, src).then_inc(ld_bhi, 16)
            for s in range(NP):
                a_slot(0, s, first=True)
                if s == 1:
                    pool.wait_ge(ld_bhi, 16 * len(B_CHUNKS))
                if 1 <= s < 1 + len(B_CHUNKS):
                    _, hi, lo = B_CHUNKS[s - 1]
                    raw = raw_b[:, :] if len(hi.shape) == 2 else raw_b[:, :].rearrange("p (a d) -> p a d", d=hi.shape[2])
                    pool.wait_ge(ld_raw, 16 * s)
                    nc.gpsimd.tensor_tensor(lo, raw, hi.bitcast(F32), ALU.subtract).then_inc(wb_lo, 1)
            with pool.Fori(1, G) as g:
                for s in range(NP):
                    a_slot(g, s)
            a_weights(NP * G - 1)

            def b_weights(n):
                wait(pool, b_rs, n + 1)
                wait(pool, b_T, n)
                nc.gpsimd.sem_inc(g_tick, 1)
                for t in range(8):
                    i = nc.gpsimd.tensor_scalar(p_f[:, t, :], e_sb[:, t, :], rsum[:, t:t + 1], 0.0, ALU.mult, ALU.add)
                i.then_inc(b_p, 1)

            def b_slot(g, s, first=False):
                if not (first and s == 0):
                    b_weights(NP * g + s - 1)
                if s == 4:
                    inv_std(G + g + 1)

            pool.wait_ge(a_x, 2 * G)
            for s in range(NP):
                b_slot(0, s, first=True)
                if s == 1:
                    pool.wait_ge(ld_cw, 16 * 6)
                    nc.gpsimd.memset(lb1[:, :, :, 1, :], 0.0).then_inc(g_lb, 1)
                    for j in range(3):
                        nc.gpsimd.tensor_copy(lb1[:, :, j, 0, :], lb_raw[:, :, 0, :]).then_inc(g_lb, 1)
                        nc.gpsimd.tensor_scalar(lb2[:, :, j, 0, :], lb_raw[:, :, 0, :], -1.0, 0.0, ALU.mult,
                                                ALU.add).then_inc(g_lb, 1)
                        nc.gpsimd.tensor_copy(lb2[:, :, j, 1, :], lb_raw[:, :, 1, :]).then_inc(g_lb, 1)
            with pool.Fori(1, G) as g:
                for s in range(NP):
                    b_slot(g, s)
            b_weights(NP * G - 1)
            for g in range(G):
                inv_std(2 * G + g + 1)

        @block.tensor
        def _(pe):
            def split3(out_, w_pair, m_pair, first, last, **kw):
                (wh, wl), (mh, ml) = w_pair, m_pair
                pe.matmul(out_, wl, mh, start=first, stop=False, **kw)
                pe.matmul(out_, wh, ml, start=False, stop=False, **kw)
                return pe.matmul(out_, wh, mh, start=False, stop=last, **kw)

            pe.wait_ge(g_const, 4)
            for n, (what, t, kt) in enumerate(PREP):
                if what == "qkv":
                    if t % 8 == 0 and kt == 0:
                        pe.wait_ge((ld_wq, ld_wk, ld_wv)[t // 8], 16)
                elif t == 0:
                    pe.wait_ge(ld_wp, 16)
                wait(pe, w_lo, n - 7)
                for j in range(4):
                    if what == "qkv":
                        src = wqkv_raw[:, t + j, kt * P:(kt + 1) * P]
                    else:
                        src = wp_raw[:, j % 2, (t + j // 2) * P:(t + j // 2 + 1) * P]
                    last = pe.transpose(banks[n % 8][:, j * P:(j + 1) * P], src, ident[:, :])
                last.then_inc(w_T, 1)
            pe.wait_ge(w_lo, len(PREP))
            pe.wait_ge(idb, 1)

            def normed_T(n, prev_reads):
                wait(pe, ln_xn, n + 1)
                prev_reads()
                for kt in range(KD):
                    for b in range(GB):
                        last = pe.transpose(proj_ps[kt][:, b * P:(b + 1) * P], xn[:, b, kt * P:(kt + 1) * P],
                                            ident[:, :])
                    last.then_inc(ln_T, 1)

            def a_block(g, m, w0, moving_tokens):
                if m < 2:
                    wait(pe, ln_lo, 2 * g + 2)
                else:
                    wait(pe, a_ri, BLOCKS * g + m - 1)
                ps = proj_ps[m % 2]
                for kt in range(KD):
                    if moving_tokens:
                        wp = [w[:, kt, w0:w0 + P] for w in (wqkvT_hi, wqkvT_lo)]
                        mp = [t[:, kt, :] for t in (xnT_hi, xnT_lo)]
                    else:
                        b, col = w0
                        wp = [t[:, kt, b * P:(b + 1) * P] for t in (xnT_hi, xnT_lo)]
                        mp = [w[:, kt, col:col + 512] for w in (wqkvT_hi, wqkvT_lo)]
                    last = split3(ps[:, :], wp, mp, kt == 0, kt == KD - 1)
                last.then_inc(a_blk, 1)

            def a_transpose(n, p):
                wait(pe, a_p, n + 1)
                wait(pe, a_aT, n)
                for t in range(8):
                    last = pe.transpose(t_ps[:, t * 64:(t + 1) * 64].bitcast(BF16),
                                        p_int[:, t, :].bitcast(BF16), ident_b[:, :])
                last.then_inc(a_T, 1)

            def a_attend(n, p, v_count):
                wait(pe, a_aT, n + 1)
                wait(pe, a_fx, v_count)
                wait(pe, a_oi, n)
                for b in range(GB):
                    for hh in range(2):
                        h0 = (2 * p + hh) * DH
                        last = pe.matmul(o_ps[hh * DH:(hh + 1) * DH, b * P:(b + 1) * P], v_sb[:, b, h0:h0 + DH],
                                         aT_sb[:, GB * hh + b, :], start=True, stop=True)
                last.then_inc(a_av, 1)

            def project_out(n, p, ready, done, weights, y_free):
                wait(pe, ready, n + 1)
                if p == 0:
                    wait(pe, *y_free)
                for b in range(GB):
                    first = p == 0 and b % 2 == 0
                    last = split3(y_ps[b // 2][:, (b % 2) * D:(b % 2 + 1) * D],
                                  [t[:, b * P:(b + 1) * P] for t in (oT_hi, oT_lo)],
                                  [w[:, p, :] for w in weights], first, p == NP - 1, skip_group_check=True)
                last.then_inc(done, 1)

            def a_scores(n, s, blk):
                wait(pe, a_fx, blk)
                wait(pe, a_y, 2 * n)
                for b in range(GB):
                    for hh in range(2):
                        last = pe.matmul(s_ps[hh][:, b * P:(b + 1) * P],
                                         q_sb[hh * DH:(hh + 1) * DH, s % 2, b * P:(b + 1) * P],
                                         k_sb[hh * DH:(hh + 1) * DH, s % 2, b * P:(b + 1) * P],
                                         start=True, stop=True)
                        if b == GB - 1:
                            last.then_inc(a_S, 1)

            def a_slot(g, s, first=False, drain=False):
                n = NP * g + s
                base = block_index(s)
                if s == 0 and not drain:
                    normed_T(g, lambda: wait(pe, a_ri, BLOCKS * g))
                if s > 0 and not drain:
                    a_block(g, base, s * P, True)
                    a_block(g, base + 1, E + s * P, True)
                if not (first and s < 2) and not (drain and s >= 2):
                    a_transpose(n - 2, (s - 2) % NP)
                if not (first and s < 3):
                    p = (s - 3) % NP
                    project_out(n - 3, p, a_olo, a_pj, (wpT_hi, wpT_lo), (a_z, 2 * g))
                if s == 0 and not drain:
                    a_block(g, base, s * P, True)
                    a_block(g, base + 1, E + s * P, True)
                if not (first and s < 2) and not (drain and s >= 2):
                    p = (s - 2) % NP
                    gg = g if s >= 2 else g - 1
                    a_attend(n - 2, p, BLOCKS * gg + (block_index(1) + 4 if p < 4 else block_index(3) + 4))
                if s < 4 and not drain:
                    for i in range(2):
                        j = 2 * s + i
                        a_block(g, base + 2 + i, (j % 4, 2 * E + 512 * (j // 4)), False)
                if not drain:
                    a_scores(n, s, BLOCKS * g + base + 2)

            for s in range(NP):
                a_slot(0, s, first=True)
            with pe.Fori(1, G) as g:
                for s in range(NP):
                    a_slot(g, s)
            for s in range(3):
                a_slot(G, s, drain=True)

            pe.wait_ge(a_x, 2 * G)
            pe.wait_ge(wb_lo, len(B_CHUNKS))

            def b_block(g, s, what, i=0):
                if what == "q":
                    wait(pe, ln_lo, 2 * (G + g) + 2)
                    if s == 0:
                        wait(pe, b_clo, g + 1)
                    elif s <= 4:
                        wait(pe, b_v, 8 * g + 2 * s)
                    else:
                        wait(pe, b_k, NP * g + s)
                    for kt in range(KD):
                        last = split3(one_ps[:, :], [w[:, kt, s * P:(s + 1) * P] for w in (wq_hi, wq_lo)],
                                      [t[:, kt, :] for t in (xnT_hi, xnT_lo)], kt == 0, kt == KD - 1)
                elif what == "k":
                    if s < 4:
                        wait(pe, b_v, 8 * g + 2 * s + 1)
                    else:
                        wait(pe, b_q, NP * g + s + 1)
                    last = split3(one_ps[:, :], [w[:, s * P:(s + 1) * P] for w in (wk_hi, wk_lo)],
                                  [t[:, :] for t in (cT_hi, cT_lo)], True, True)
                else:
                    if i == 0:
                        wait(pe, b_q, NP * g + s + 1)
                    else:
                        wait(pe, b_k, NP * g + s + 1)
                    b, col = (2 * s + i) % 4, 512 * ((2 * s + i) // 4)
                    last = split3(one_ps[:, :], [t[:, b * P:(b + 1) * P] for t in (cT_hi, cT_lo)],
                                  [w[:, col:col + 512] for w in (wv_hi, wv_lo)], True, True)
                last.then_inc(b_blk, 1)

            def b_transpose(n):
                wait(pe, b_p, n + 1)
                wait(pe, b_pT, n)
                for hh in range(2):
                    for b in range(GB):
                        last = pe.transpose(pT_ps[hh][:, b * P:(b + 1) * P], p_f[:, GB * hh + b, :], ident[:, :])
                last.then_inc(b_T, 1)

            def b_attend(n, p, v_count):
                wait(pe, b_pT, n + 1)
                wait(pe, b_v, v_count)
                wait(pe, b_olo, n)
                for b in range(GB):
                    for hh in range(2):
                        h0 = (2 * p + hh) * DH
                        last = pe.matmul(o_ps[hh * DH:(hh + 1) * DH, b * P:(b + 1) * P], v_sb[:, b, h0:h0 + DH],
                                         aT_sb[:, GB * hh + b, :], start=True, stop=True)
                last.then_inc(b_av, 1)

            def b_scores(g, n, s):
                wait(pe, b_q, n + 1)
                wait(pe, b_k, n + 1)
                wait(pe, b_e, n)
                for b in range(GB):
                    for hh in range(2):
                        last = pe.matmul(s_ps[hh][:, b * P:(b + 1) * P],
                                         q_sb[hh * DH:(hh + 1) * DH, s % 2, b * P:(b + 1) * P],
                                         k_sb[hh * DH:(hh + 1) * DH, s % 2, b * P:(b + 1) * P],
                                         start=True, stop=True)
                        if b == GB - 1:
                            last.then_inc(b_S, 1)

            def b_slot(g, s, first=False, drain=False):
                n = NP * g + s
                lag2 = not (first and s < 2) and not (drain and s >= 2)
                if s == 0 and not drain:
                    def free():
                        wait(pe, b_k, NP * g)
                        wait(pe, b_pT, n - 2)
                    normed_T(G + g, free)
                    wait(pe, ld_ctx, 16 * (g + 1))
                    wait(pe, ln_lo, 2 * (G + g) + 1)
                    for b in range(GB):
                        last = pe.transpose(one_ps[:, b * P:(b + 1) * P], ctx_sb[:, b, :], ident[:, :])
                    last.then_inc(b_cT, 1)
                if s > 0 and not drain:
                    b_block(g, s, "q")
                if lag2:
                    if s == 0 and not drain:
                        wait(pe, ln_lo, 2 * (G + g) + 2)
                    b_transpose(n - 2)
                if s > 0 and s < 4 and not drain:
                    b_block(g, s, "v", 0)
                if not (first and s < 3):
                    project_out(n - 3, (s - 3) % NP, b_olo, b_pj, (wo_hi, wo_lo), (b_z, 2 * g))
                if not drain:
                    if s == 0:
                        b_block(g, s, "q")
                        b_block(g, s, "v", 0)
                    b_block(g, s, "k")
                if lag2:
                    p = (s - 2) % NP
                    gg = g if s >= 2 else g - 1
                    b_attend(n - 2, p, 8 * gg + (4 if p < 4 else 8))
                if not drain:
                    if s < 4:
                        b_block(g, s, "v", 1)
                    b_scores(g, n, s)

            for s in range(NP):
                b_slot(0, s, first=True)
            with pe.Fori(1, G) as g:
                for s in range(NP):
                    b_slot(g, s)
            for s in range(3):
                b_slot(G, s, drain=True)

            pe.wait_ge(b_x, 2 * G)
            pe.wait_ge(g_lb, 10)
            for n, (what, t, kt) in enumerate(C_PREP):
                wait(pe, cw_lo, n - 7)
                for j in range(4):
                    if what == "up":
                        last = pe.transpose(banks[n % 8][:, j * P:(j + 1) * P], wi_raw[:, t + j, kt * P:(kt + 1) * P],
                                            ident[:, :])
                    elif what == "down":
                        f0 = (t + j // 2) * P
                        last = pe.transpose(banks[n % 8][:, j * P:(j + 1) * P], wd_raw[:, j % 2, f0:f0 + P], ident[:, :])
                    elif what in ("lb1", "lb2"):
                        src = (lb1 if what == "lb1" else lb2)[:, t + j, :, :, :].rearrange("p c k r -> p (c k r)")
                        last = pe.transpose(banks[n % 8][0:96, j * P:(j + 1) * P], src, ident[:, :])
                    elif j < KD:
                        last = pe.transpose(banks[n % 8][:, j * 32:(j + 1) * 32], la_raw[:, j * P:(j + 1) * P],
                                            ident[0:32, 0:32])
                last.then_inc(cw_T, 1)
            pe.wait_ge(cw_lo, len(C_PREP))

            def c_slot(g, s, first=False, drain=False):
                n = NF * g + s
                if s == 0 and not drain:
                    normed_T(2 * G + g, lambda: wait(pe, c_tlo, g))
                def up():
                    wait(pe, c_r1, n - 3)
                    u = up_ps[s % 4]
                    for kt in range(KD):
                        split3(u[:, :], [w[:, kt, s * P:(s + 1) * P] for w in (wiT_hi, wiT_lo)],
                               [t[:, kt, :] for t in (xnT_hi, xnT_lo)], kt == 0, False)
                    wait(pe, c_tlo, g + 1)
                    pe.matmul(u[:, :], lb1T[:, s * P:(s + 1) * P], lowT[:, :], start=False, stop=True).then_inc(c_u, 1)
                if not drain and s > 0:
                    up()
                if not (first and s < 1) and not (drain and s >= 1):
                    p = (s - 1) % NF
                    wait(pe, c_g0, n)
                    pe.matmul(up_ps[p % 4][:, :], lb2T[:, p * P:(p + 1) * P], lowT[:, :], start=False, stop=True,
                              skip_group_check=True).then_inc(c_u2, 1)
                if not (first and s < 2):
                    p = (s - 2) % NF
                    wait(pe, c_glo, n - 1)
                    if p == 0:
                        wait(pe, c_x, 2 * g)
                    for b in range(GB):
                        last = split3(y_ps[b // 2][:, (b % 2) * D:(b % 2 + 1) * D],
                                      [t[:, b * P:(b + 1) * P] for t in (oT_hi, oT_lo)],
                                      [w[:, p, :] for w in (wdT_hi, wdT_lo)], p == 0 and b % 2 == 0, p == NF - 1,
                                      skip_group_check=True)
                    last.then_inc(c_dn, 1)
                if s == 0 and not drain:
                    wait(pe, ln_lo, 2 * (2 * G + g) + 2)
                    for kt in range(KD):
                        last = split3(low_ps[:, :], [w[:, kt, :] for w in (laT_hi, laT_lo)],
                                      [t[:, kt, :] for t in (xnT_hi, xnT_lo)], kt == 0, kt == KD - 1)
                    last.then_inc(c_t, 1)
                    up()

            for s in range(NF):
                c_slot(0, s, first=True)
            with pe.Fori(1, G) as g:
                for s in range(NF):
                    c_slot(g, s)
            for s in range(2):
                c_slot(G, s, drain=True)

        @block.scalar
        def _(act):
            for n, (what, t, kt) in enumerate(PREP):
                act.wait_ge(w_T, n + 1)
                dst = wqkvT_hi[:, kt, t * P:t * P + 512] if what == "qkv" else wpT_hi[:, t:t + 2, :].rearrange("p a d -> p (a d)")
                nc.scalar.copy(dst, banks[n % 8][:, :]).then_inc(w_hi, 1)

            def xnT_high(n, scale):
                for kt in range(KD):
                    wait(act, ln_T, 2 * n + kt + 1)
                    nc.scalar.activation(xnT_hi[:, kt, :], proj_ps[kt][:, :], ACT.Copy,
                                         scale=scale).then_inc(ln_hi, 1)

            def sign_of(g, m):
                wait(act, a_blk, BLOCKS * g + m + 1)
                wait(act, a_ri, BLOCKS * g + m - 1)
                nc.scalar.activation(sgn[:, m % 2, :], proj_ps[m % 2][:, :], ACT.Sign).then_inc(a_sgn, 1)

            def a_slot(g, s, first=False, drain=False):
                n = NP * g + s
                base = block_index(s)
                if not drain:
                    if s == 0:
                        xnT_high(g, FIX * GROW)
                    if s > 0:
                        sign_of(g, base)
                        sign_of(g, base + 1)
                lag2 = not (first and s < 2) and not (drain and s >= 2)
                if lag2:
                    wait(act, a_T, n - 1)
                    wait(act, a_av, n - 2)
                    nc.scalar.activation(aT_sb[:, :, :].rearrange("p a t -> p (a t)"), t_ps[:, :].bitcast(I16),
                                         ACT.Copy, scale=1.0 / FIX).then_inc(a_aT, 1)
                if not drain and s == 0:
                    sign_of(g, base)
                    sign_of(g, base + 1)
                if (not (first and s == 0)) and not (drain and s >= 1):
                    wait(act, a_p, n - 1)
                    wait(act, a_rs, n - 1)
                    for i in range(2):
                        wait(act, a_clip, 2 * n - 1 + i)
                        for j in range(4):
                            t = 4 * i + j
                            last = nc.scalar.activation(e_sb[:, t, :], si[:, i, j * P:(j + 1) * P], ACT.Exp,
                                                        scale=1.0 / FIX, accum_out=sums[:, t:t + 1])
                        last.then_inc(a_e, 1)
                if not drain:
                    if s < 4:
                        sign_of(g, base + 2)
                        sign_of(g, base + 3)
                if lag2:
                    wait(act, a_oi, n - 1)
                    wait(act, a_pj, n - 2)
                    nc.scalar.copy(oT_hi[:, :], oi[:, :]).then_inc(a_ohi, 1)
                if not drain:
                    for i in range(2):
                        wait(act, a_S, 2 * n + i + 1)
                        wait(act, a_si, 2 * n + i - 1)
                        nc.scalar.copy(y_sb[:, i, :], s_ps[i][:, :]).then_inc(a_y, 1)

            for s in range(NP):
                a_slot(0, s, first=True)
            with act.Fori(1, G) as g:
                for s in range(NP):
                    a_slot(g, s)
            for s in range(2):
                a_slot(G, s, drain=True)

            act.wait_ge(a_x, 2 * G)

            def b_slot(g, s, first=False, drain=False):
                n = NP * g + s
                lag2 = not (first and s < 2) and not (drain and s >= 2)
                if not drain:
                    if s == 0:
                        xnT_high(G + g, 1.0)
                        wait(act, b_cT, g + 1)
                        nc.scalar.copy(cT_hi[:, :], one_ps[:, :]).then_inc(b_chi, 1)
                    wait(act, b_S, 2 * n - 2)
                    wait(act, b_blk, BLOCKS * g + block_index(s) + 1)
                    nc.scalar.copy(q_sb[:, s % 2, :], one_ps[:, :]).then_inc(b_q, 1)
                if (not (first and s == 0)) and not (drain and s >= 1):
                    wait(act, b_p, n - 1)
                    wait(act, b_rs, n - 1)
                    for hh in range(2):
                        wait(act, b_nm, 2 * n - 1 + hh)
                        for t in range(GB * hh, GB * hh + GB):
                            last = nc.scalar.activation(e_sb[:, t, :], s_ps[hh][:, (t % 4) * P:(t % 4 + 1) * P], ACT.Exp,
                                                        bias=neg_max[:, t:t + 1], scale=DH ** -0.5,
                                                        accum_out=sums[:, t:t + 1])
                    last.then_inc(b_e, 1)
                if lag2:
                    wait(act, b_av, n - 1)
                    wait(act, b_pj, n - 2)
                    nc.scalar.copy(oT_hi[:, :], o_ps[:, :]).then_inc(b_ohi, 1)

            for s in range(NP):
                b_slot(0, s, first=True)
            with act.Fori(1, G) as g:
                for s in range(NP):
                    b_slot(g, s)
            for s in range(2):
                b_slot(G, s, drain=True)

            act.wait_ge(b_x, 2 * G)
            for n, (what, t, kt) in enumerate(C_PREP):
                act.wait_ge(cw_T, n + 1)
                bank = banks[n % 8]
                if what == "up":
                    last = nc.scalar.copy(wiT_hi[:, kt, t * P:t * P + 512], bank[:, :])
                elif what == "down":
                    last = nc.scalar.copy(wdT_hi[:, t:t + 2, :].rearrange("p a d -> p (a d)"), bank[:, :])
                elif what in ("lb1", "lb2"):
                    last = nc.scalar.copy((lb1T if what == "lb1" else lb2T)[:, t * P:t * P + 512], bank[0:96, :])
                else:
                    for j in range(4):
                        last = nc.scalar.copy(laT_hi[:, :, 32 * j:32 * j + 32],
                                              bank[:, 0:64].rearrange("p (k r) -> p k r", k=KD))
                last.then_inc(cw_hi, 1)

            def c_slot(g, s, first=False, drain=False):
                n = NF * g + s
                if s == 0 and not drain:
                    xnT_high(2 * G + g, 1.0)
                if not (first and s < 1) and not (drain and s >= 1):
                    p = (s - 1) % NF
                    wait(act, c_u2, n)
                    wait(act, c_g, n - 1)
                    nc.scalar.activation(relu1[:, :], up_ps[p % 4][:, :], ACT.Relu).then_inc(c_r1, 1)
                    wait(act, c_g, n)
                    wait(act, c_dn, n - 1)
                    nc.scalar.copy(oT_hi[:, :], hid[:, :]).then_inc(c_ghi, 1)
                if s == 0 and not drain:
                    wait(act, c_t, g + 1)
                    nc.scalar.copy(lowT[:, :], low_ps[0:96, :]).then_inc(c_thi, 1)

            for s in range(NF):
                c_slot(0, s, first=True)
            with act.Fori(1, G) as g:
                for s in range(NF):
                    c_slot(g, s)
            c_slot(G, 0, drain=True)

        @block.vector
        def _(dve):
            V = nc.vector

            def norm_stats(n, g):
                for b in range(GB):
                    i = V.bn_stats(bn_st[:, b, :], x_sb[:, bass.ds(g * GB + b, 1), :].rearrange("p a d -> p (a d)"))
                i.then_inc(ln_bn, 1)

            def add_rows(gp, j, z, done):
                xx = x_sb[:, bass.ds(gp * GB + 2 * j, 2), :].rearrange("p a d -> p (a d)")
                V.tensor_tensor(xx, xx, z, ALU.add).then_inc(done, 1)

            def norm_moments():
                for b in range(GB):
                    i = V.bn_aggr(mv[:, b, :], bn_st[:, b, :])
                i.then_inc(ln_mv, 1)

            def norm_apply(n, g, T_count):
                wait(dve, T_count[0], T_count[1])
                wait(dve, g_rstd, n + 1)
                for b in range(GB):
                    i = V.tensor_scalar(xn[:, b, :], x_sb[:, bass.ds(g * GB + b, 1), :].rearrange("p a d -> p (a d)"),
                                        mv[:, b, 0:1], rstd[:, b:b + 1], ALU.subtract, ALU.mult)
                i.then_inc(ln_xn, 1)

            dve.wait_ge(ld_x0, 16)
            norm_stats(0, 0)
            dve.wait_ge(ln_bn, 1)
            norm_moments()
            norm_apply(0, 0, (ln_T, 0))
            dve.wait_ge(g_const, 4)
            V.tensor_copy(ident_b[:, :], ident[:, :]).then_inc(idb, 1)
            for n, (what, t, kt) in enumerate(PREP):
                dve.wait_ge(w_hi, n + 1)
                if what == "qkv":
                    hi, lo = (w[:, kt, t * P:t * P + 512] for w in (wqkvT_hi, wqkvT_lo))
                else:
                    hi, lo = (w[:, t:t + 2, :].rearrange("p a d -> p (a d)") for w in (wpT_hi, wpT_lo))
                V.tensor_tensor(lo, banks[n % 8][:, :], hi.bitcast(F32), ALU.subtract).then_inc(w_lo, 1)
            dve.wait_ge(ld_b, 16)
            dve.wait_ge(ld_xr, 48)
            V.tensor_scalar(bias_a[:, :], bias_a[:, :], FIX, None, ALU.mult).then_inc(idb, 1)

            def xnT_low(n, scale):
                for kt in range(KD):
                    wait(dve, ln_hi, 2 * n + kt + 1)
                    V.scalar_tensor_tensor(xnT_lo[:, kt, :], proj_ps[kt][:, :], scale, xnT_hi[:, kt, :].bitcast(F32),
                                           ALU.mult, ALU.subtract).then_inc(ln_lo, 1)

            def fix_blocks(g, m, dsts, scales):
                for i in range(2):
                    wait(dve, a_sgn, BLOCKS * g + m + i + 1)
                    wait(dve, a_fx, BLOCKS * g + m + i - 1)
                    V.scalar_tensor_tensor(ri[:, i, :], sgn[:, i, :], -0.5, proj_ps[i][:, :],
                                           ALU.mult, ALU.add).then_inc(a_ri, 1)
                for i in range(2):
                    wait(dve, a_ri, BLOCKS * g + m + i + 1)
                    V.tensor_scalar(dsts[i], ri[:, i, :], LOW, scales[i], ALU.max, ALU.mult).then_inc(a_fx, 1)

            def qk(g, s, n):
                wait(dve, a_S, 2 * n - 2)
                m = block_index(s)
                fix_blocks(g, m, (q_sb[:, s % 2, :], k_sb[:, s % 2, :]), (1.0 / (FIX * DH ** 0.5), 1.0))

            def a_out(n):
                wait(dve, a_av, n + 1)
                V.tensor_scalar(near0[:, 0, :], o_ps[:, :], 0.5, -0.5, ALU.min, ALU.max).then_inc(a_onear, 1)
                wait(dve, a_onear, n + 1)
                V.scalar_tensor_tensor(oi[:, :], o_ps[:, :], GROW, near0[:, 0, :], ALU.mult,
                                       ALU.subtract).then_inc(a_oi, 1)

            def a_slot(g, s, first=False, drain=False):
                n = NP * g + s
                base = block_index(s)
                lag2 = not (first and s < 2) and not (drain and s >= 2)
                if not drain:
                    if s == 0:
                        xnT_low(g, FIX * GROW)
                    if s == 4:
                        wait(dve, ln_bn, g + 2)
                    qk(g, s, n)
                if lag2:
                    a_out(n - 2)
                if (not (first and s == 0)) and not (drain and s >= 1):
                    wait(dve, a_e, 2 * n)
                    wait(dve, a_p, n - 1)
                    V.reciprocal(rsum[:, :], sums[:, :]).then_inc(a_rs, 1)
                if not drain and s < 4:
                    if s == 0 and not first:
                        wait(dve, a_av, NP * g - 4)
                    if s == 2:
                        wait(dve, a_av, NP * g)
                    fix_blocks(g, base + 2, [v_sb[:, j % 4, 512 * (j // 4):512 * (j // 4) + 512]
                                             for j in (2 * s, 2 * s + 1)], (1.0, 1.0))
                if lag2:
                    wait(dve, a_ohi, n - 1)
                    V.tensor_tensor(oT_lo[:, :], oi[:, :], oT_hi[:, :].bitcast(F32), ALU.subtract).then_inc(a_olo, 1)
                if not drain:
                    for i in range(2):
                        wait(dve, a_y, 2 * n + i + 1)
                        V.tensor_scalar(near0[:, i, :], y_sb[:, i, :], 0.5, -0.5, ALU.min, ALU.max).then_inc(a_near, 1)
                    for i in range(2):
                        wait(dve, a_near, 2 * n + i + 1)
                        V.scalar_tensor_tensor(si[:, i, :], y_sb[:, i, :], GROW, near0[:, i, :], ALU.mult,
                                               ALU.subtract).then_inc(a_si, 1)
                    for i in range(2):
                        wait(dve, a_si, 2 * n + i + 1)
                        V.tensor_scalar(si[:, i, :], si[:, i, :], LOW, None, ALU.max).then_inc(a_clip, 1)
                if s == 2 and not first:
                    wait(dve, a_pj, NP * g)
                    dve.wait_ge(wb_lo, len(B_CHUNKS))
                    bias = bias_a[:, :].rearrange("p (a d) -> p a d", a=1).broadcast_to([P, 2, D])
                    for j in range(2):
                        V.tensor_tensor(raw_b[:, j * TOK:(j + 1) * TOK].rearrange("p (a d) -> p a d", a=2),
                                        y_ps[j][:, :].rearrange("p (a d) -> p a d", a=2), bias, ALU.add).then_inc(a_z, 1)
                if not first and (s in (4, 5) or drain and s == 2):
                    for j in (0, 1) if drain else (s - 4,):
                        z, near = raw_b[:, j * TOK:(j + 1) * TOK], near0[:, j, :]
                        count = 2 * (g - 1) + j + 1
                        wait(dve, a_z, count)
                        V.tensor_scalar(near, z, 0.5, -0.5, ALU.min, ALU.max).then_inc(a_zn, 1)
                        wait(dve, a_zn, count)
                        wait(dve, a_fx, BLOCKS * g + (0 if drain else block_index(s + 1)))
                        V.scalar_tensor_tensor(ri[:, j, :], z, GROW, near, ALU.mult, ALU.subtract).then_inc(a_zi, 1)
                        wait(dve, a_zi, count)
                        V.tensor_scalar(near, ri[:, j, :], LOW, 1.0 / FIX, ALU.max, ALU.mult).then_inc(a_zf, 1)
                        wait(dve, a_zf, count)
                        if s == 5:
                            wait(dve, a_x, 2 * g - 1)
                        add_rows(g - 1, j, near, a_x)
                if not drain and s == 3:
                    norm_stats(g + 1, (g + 1) % G)
                if not drain and s == 4:
                    norm_moments()
                if not drain and s == 5:
                    norm_apply(g + 1, (g + 1) % G, (ln_T, 2 * g + 2))

            for s in range(NP):
                a_slot(0, s, first=True)
            with dve.Fori(1, G) as g:
                for s in range(NP):
                    a_slot(g, s)
            for s in range(3):
                a_slot(G, s, drain=True)

            dve.wait_ge(ld_bb, 16)
            dve.wait_ge(a_x, 2 * G)

            def b_slot(g, s, first=False, drain=False):
                n = NP * g + s
                lag2 = not (first and s < 2) and not (drain and s >= 2)
                if not drain:
                    if s == 0:
                        xnT_low(G + g, 1.0)
                        wait(dve, b_chi, g + 1)
                        V.tensor_tensor(cT_lo[:, :], one_ps[:, :], cT_hi[:, :].bitcast(F32), ALU.subtract).then_inc(b_clo, 1)
                    if s == 4:
                        wait(dve, ln_bn, G + g + 2)
                if (not (first and s == 0)) and not (drain and s >= 1):
                    for hh in range(2):
                        wait(dve, b_S, 2 * n - 1 + hh)
                        half = slice(GB * hh, GB * hh + GB)
                        V.reduce_max(mx[:, half], s_ps[hh][:, :].rearrange("p (a t) -> p a t", a=GB), AX).then_inc(b_mx, 1)
                    for hh in range(2):
                        half = slice(GB * hh, GB * hh + GB)
                        wait(dve, b_mx, 2 * n - 1 + hh)
                        V.tensor_scalar(neg_max[:, half], mx[:, half], -DH ** -0.5, None, ALU.mult).then_inc(b_nm, 1)
                if lag2:
                    wait(dve, b_T, n - 1)
                    wait(dve, b_av, n - 2)
                    for hh in range(2):
                        i = V.tensor_copy(aT_sb[:, GB * hh:GB * hh + GB, :].rearrange("p a t -> p (a t)"),
                                          pT_ps[hh][:, :])
                    i.then_inc(b_pT, 1)
                if s == 4 and not drain:
                    norm_moments()

                def v_rows(i):
                    j = 2 * s + i
                    wait(dve, b_blk, BLOCKS * g + block_index(s) + 2 + 2 * i)
                    V.tensor_copy(v_sb[:, j % 4, 512 * (j // 4):512 * (j // 4) + 512], one_ps[:, :]).then_inc(b_v, 1)

                if not drain:
                    if s == 0 and not first:
                        wait(dve, b_av, NP * g - 4)
                    if s == 2:
                        wait(dve, b_av, NP * g)
                    if s < 4:
                        v_rows(0)
                    wait(dve, b_S, 2 * n - 2)
                    wait(dve, b_blk, BLOCKS * g + block_index(s) + (3 if s < 4 else 2))
                    V.tensor_copy(k_sb[:, s % 2, :], one_ps[:, :]).then_inc(b_k, 1)
                if (not (first and s == 0)) and not (drain and s >= 1):
                    wait(dve, b_e, n)
                    wait(dve, b_p, n - 1)
                    V.reciprocal(rsum[:, :], sums[:, :]).then_inc(b_rs, 1)
                if not drain and s < 4:
                    v_rows(1)
                if lag2:
                    wait(dve, b_ohi, n - 1)
                    V.tensor_tensor(oT_lo[:, :], o_ps[:, :], oT_hi[:, :].bitcast(F32), ALU.subtract).then_inc(b_olo, 1)
                if s == 2 and not first:
                    wait(dve, b_pj, NP * g)
                    bias = bias_b[:, :].rearrange("p (a d) -> p a d", a=1).broadcast_to([P, 2, D])
                    for j in range(2):
                        V.tensor_tensor(near0[:, j, :].rearrange("p (a d) -> p a d", a=2),
                                        y_ps[j][:, :].rearrange("p (a d) -> p a d", a=2), bias, ALU.add).then_inc(b_z, 1)
                    wait(dve, b_z, 2 * g)
                    for j in range(2):
                        add_rows(g - 1, j, near0[:, j, :], b_x)
                if not drain and s == 3:
                    wait(dve, b_x, 2 * g)
                    norm_stats(G + g + 1, (g + 1) % G)
                if not drain and s == 5:
                    norm_apply(G + g + 1, (g + 1) % G, (ln_T, 2 * (G + g) + 2))

            for s in range(NP):
                b_slot(0, s, first=True)
            with dve.Fori(1, G) as g:
                for s in range(NP):
                    b_slot(g, s)
            for s in range(3):
                b_slot(G, s, drain=True)

            dve.wait_ge(ld_top, 16)
            dve.wait_ge(b_x, 2 * G)
            for n, (what, t, kt) in enumerate(C_PREP):
                dve.wait_ge(cw_hi, n + 1)
                bank = banks[n % 8]
                if what == "up":
                    i = V.tensor_tensor(wiT_lo[:, kt, t * P:t * P + 512], bank[:, :],
                                        wiT_hi[:, kt, t * P:t * P + 512].bitcast(F32), ALU.subtract)
                elif what == "down":
                    lo, hi = (w[:, t:t + 2, :].rearrange("p a d -> p (a d)") for w in (wdT_lo, wdT_hi))
                    i = V.tensor_tensor(lo, bank[:, :], hi.bitcast(F32), ALU.subtract)
                elif what in ("lb1", "lb2"):
                    third = (lb1T if what == "lb1" else lb2T)[64:96, t * P:t * P + 512]
                    i = V.tensor_tensor(third, bank[64:96, :], third.bitcast(F32), ALU.subtract)
                else:
                    for j in range(4):
                        i = V.tensor_tensor(laT_lo[:, :, 32 * j:32 * j + 32],
                                            bank[:, 0:64].rearrange("p (k r) -> p k r", k=KD),
                                            laT_hi[:, :, 32 * j:32 * j + 32].bitcast(F32), ALU.subtract)
                i.then_inc(cw_lo, 1)

            def c_slot(g, s, first=False, drain=False):
                n = NF * g + s
                if not drain:
                    if s == 0:
                        xnT_low(2 * G + g, 1.0)
                    if s == 4:
                        wait(dve, ln_bn, 2 * G + g + 2)
                    if s > 0:
                        c_expert0(g, s, n)
                    if s == 4:
                        norm_moments()
                if not (first and s < 1) and not (drain and s >= 1):
                    p = (s - 1) % NF
                    wait(dve, c_r1, n)
                    wait(dve, c_glo, n - 1)
                    V.scalar_tensor_tensor(hid[:, :], relu1[:, :], top_sb[:, 1:2], hid0[:, p % 2, :], ALU.mult,
                                           ALU.add).then_inc(c_g, 1)
                    wait(dve, c_ghi, n)
                    V.tensor_tensor(oT_lo[:, :], hid[:, :], oT_hi[:, :].bitcast(F32), ALU.subtract).then_inc(c_glo, 1)
                if not drain and s == 0:
                    wait(dve, c_thi, g + 1)
                    V.tensor_tensor(lowT[32:64, :], low_ps[32:64, :], lowT[32:64, :].bitcast(F32),
                                    ALU.subtract).then_inc(c_tlo, 1)
                    c_expert0(g, s, n)
                if s == 1 and not first:
                    wait(dve, c_dn, NF * g)
                    for j in range(2):
                        add_rows(g - 1, j, y_ps[j][:, :], c_x)
                if not drain and s == 3:
                    norm_stats(2 * G + g + 1, (g + 1) % G)
                if not drain and s == 5:
                    norm_apply(2 * G + g + 1, (g + 1) % G, (ln_T, 2 * (2 * G + g) + 2))

            def c_expert0(g, s, n):
                wait(dve, c_u, n + 1)
                V.tensor_scalar(hid0[:, s % 2, :], up_ps[s % 4][:, :], 0.0, top_sb[:, 0:1], ALU.max,
                                ALU.mult).then_inc(c_g0, 1)

            for s in range(NF):
                c_slot(0, s, first=True)
            with dve.Fori(1, G) as g:
                for s in range(NF):
                    c_slot(g, s)
            for s in range(2):
                c_slot(G, s, drain=True)


INPUTS = ["x", "ctx_512", "L0_attn_w_qkv", "L0_attn_w_proj", "L0_attn_b_proj", "L0_xattn_Wq", "L0_xattn_Wk",
          "L0_xattn_Wv", "L0_xattn_Wo", "L0_xattn_bo", "L0_ffn_wi_w", "L0_ffn_wo_w", "L0_ffn_lora_As",
          "L0_ffn_lora_Bs", "L0_ffn_top_k_indices", "L0_ffn_top_k_values"]


def kernel(**inputs):
    import concourse.bacc as bacc
    from concourse.bass_utils import run_bass_kernel_spmd

    nc = bacc.Bacc("TRN2", target_bir_lowering=False, num_devices=1)
    arrays, args = {}, []
    for name in INPUTS:
        a = np.ascontiguousarray(inputs[name])
        arrays[f"in_{name}"] = a
        args.append(nc.dram_tensor(f"in_{name}", a.shape, mybir.dt.from_np(a.dtype), kind="ExternalInput").ap())
    out = nc.dram_tensor("out", (B, NT, D), F32, kind="ExternalOutput").ap()
    build(nc, *args, out)
    r = run_bass_kernel_spmd(nc, [arrays], core_ids=[0])
    return r.results[0]["out"]
```

```python
import numpy as np
import concourse.bass as bass
from concourse import mybir
from concourse.alu_op_type import AluOpType as ALU

F32 = mybir.dt.float32
F32R = mybir.dt.float32r
BF16 = mybir.dt.bfloat16
I16 = mybir.dt.int16
I32 = mybir.dt.int32
ACT = mybir.ActivationFunctionType
AX = mybir.AxisListType.X

P = 128
B, NT, D = 16, 128, 256
H, DH = 16, 64
E = H * DH
F = 1024
CTX = 128
RANK = 16
GB = 4
G = B // GB
TOK = GB * NT
KD = D // P
NP = H // 2
NF = F // P
FIX = 4096.0
GROW = 1.0 + 2.0 ** -22
LOW = -(8.0 * FIX - 1.0)
EPS = 1e-5


def sbuf_map(nc):
    state = {"at": (nc.sbuf_base + 63) // 64 * 64}

    def place(name, shape, dtype, at=None):
        nbytes = int(np.prod(shape[1:])) * mybir.dt.size(dtype)
        nbytes = (nbytes + 31) // 32 * 32
        if at is None:
            at = state["at"]
            state["at"] = at + nbytes
        return nc.alloc_sbuf_tensor_at(name, list(shape), dtype, offset=at), at, at + nbytes

    return place, state


def block_index(s):
    return 4 * s if s < 4 else 16 + 2 * (s - 4)


BLOCKS = block_index(8)


def build(nc, x, ctx, w_qkv, w_proj, b_proj, Wq, Wk, Wv, Wo, bo, wi_w, wo_w, lora_As, lora_Bs,
          top_i, top_v, out):
    place, mem = sbuf_map(nc)

    def sb(name, shape, dtype, at=None):
        return place(name, shape, dtype, at)[0]

    x_sb = sb("x_sb", [P, B, D], F32)
    region_a = mem["at"]
    wqkvT_hi = sb("wqkvT_hi", [P, KD, 3 * E], F32R)
    wqkvT_lo = sb("wqkvT_lo", [P, KD, 3 * E], F32R)
    wpT_hi = sb("wpT_hi", [P, NP, D], F32R)
    wpT_lo = sb("wpT_lo", [P, NP, D], F32R)
    region_b = mem["at"]
    wq_hi = sb("wq_hi", [P, KD, E], F32R)
    wq_lo = sb("wq_lo", [P, KD, E], F32R)
    wk_hi = sb("wk_hi", [P, E], F32R)
    wk_lo = sb("wk_lo", [P, E], F32R)
    wv_hi = sb("wv_hi", [P, E], F32R)
    wv_lo = sb("wv_lo", [P, E], F32R)
    wo_hi = sb("wo_hi", [P, NP, D], F32R)
    wo_lo = sb("wo_lo", [P, NP, D], F32R)
    wqkv_raw, _, nxt = place("wqkv_raw", [P, 3 * NP, D], F32, at=region_b)
    wp_raw, _, nxt = place("wp_raw", [P, KD, E], F32, at=nxt)
    raw_b = sb("raw_b", [P, E], F32)
    xn = sb("xn", [P, GB, D], F32)
    xnT_hi = sb("xnT_hi", [P, KD, TOK], F32R)
    xnT_lo = sb("xnT_lo", [P, KD, TOK], F32R)
    v_sb = sb("v_sb", [P, GB, E], F32)
    q_sb = sb("q_sb", [P, 2, TOK], F32)
    k_sb = sb("k_sb", [P, 2, TOK], F32)
    e_sb = sb("e_sb", [P, 8, NT], F32)
    p_int = sb("p_int", [P, 8, NT], I16)
    y_sb = sb("y_sb", [P, 2, TOK], F32)
    aT_sb = sb("aT_sb", [P, 8, NT], F32)
    oT_hi = sb("oT_hi", [P, TOK], F32R)
    oT_lo = sb("oT_lo", [P, TOK], F32R)
    sgn = sb("sgn", [P, 2, TOK], BF16)
    ri = sb("ri", [P, 2, TOK], I16)
    near0 = sb("near0", [P, 2, TOK], F32)
    si = sb("si", [P, 2, TOK], I16)
    oi = sb("oi", [P, TOK], I16)
    zi = sb("zi", [P, TOK], I16)
    ident = sb("ident", [P, P], F32)
    ident_b = sb("ident_b", [P, P], BF16)
    bias_a = sb("bias_a", [P, D], F32)
    bn_st = sb("bn_st", [P, GB, 6], F32)
    mv = sb("mv", [P, GB, 2], F32)
    veps = sb("veps", [P, GB], F32)
    rstd = sb("rstd", [P, GB], F32)
    mhalf = sb("mhalf", [P, GB], F32)
    sums = sb("sums", [P, 8], F32)
    rsum = sb("rsum", [P, 8], F32)
    rsc = sb("rsc", [P, 8], F32)
    mx = sb("mx", [P, 8], F32)
    neg_max = sb("neg_max", [P, 8], F32)
    bias_b = sb("bias_b", [P, D], F32)
    growth = sb("growth", [P, 8], F32)
    top_sb = sb("top_sb", [P, 2], F32)

    ctx_sb, _, nxt = place("ctx_sb", [P, GB, CTX], F32, at=region_a)
    cT_hi, _, nxt = place("cT_hi", [P, TOK], F32R, at=nxt)
    cT_lo, _, nxt = place("cT_lo", [P, TOK], F32R, at=nxt)
    p_f, _, nxt = place("p_f", [P, 8, NT], F32, at=nxt)
    wi_raw, _, nxt = place("wi_raw", [P, NF, D], F32, at=nxt)
    wd_raw, _, nxt = place("wd_raw", [P, KD, F], F32, at=nxt)
    lb_raw, _, nxt = place("lb_raw", [P, NF, 2, RANK], F32, at=nxt)
    lb1, _, nxt = place("lb1", [P, NF, 3, 2, RANK], F32, at=nxt)
    lb2, _, nxt = place("lb2", [P, NF, 3, 2, RANK], F32, at=nxt)
    la_raw, _, nxt = place("la_raw", [2 * RANK, D], F32, at=nxt)
    idx_sb, _, nxt = place("idx_sb", [1, 2], I32, at=nxt)
    hid0, _, nxt = place("hid0", [P, 2, TOK], F32, at=nxt)
    relu1, _, nxt = place("relu1", [P, TOK], F32, at=nxt)
    hid, _, nxt = place("hid", [P, TOK], F32, at=nxt)
    lowT, _, nxt = place("lowT", [96, TOK], F32R, at=nxt)
    assert nxt <= region_a + 4 * KD * 3 * E * 2
    lb1T, _, nxt = place("lb1T", [96, F], F32R, at=nxt)
    lb2T, _, nxt = place("lb2T", [96, F], F32R, at=nxt)
    laT_hi, _, nxt = place("laT_hi", [P, KD, P], F32R, at=nxt)
    laT_lo, _, nxt = place("laT_lo", [P, KD, P], F32R, at=nxt)
    oT2_hi, _, nxt = place("oT2_hi", [P, TOK], F32R, at=nxt)
    oT2_lo, _, nxt = place("oT2_lo", [P, TOK], F32R, at=nxt)
    assert nxt <= region_b
    tile_hi, tile_lo = (oT_hi, oT2_hi), (oT_lo, oT2_lo)
    wiT_hi, _, nxt = place("wiT_hi", [P, KD, F], F32R, at=region_b)
    wiT_lo, _, nxt = place("wiT_lo", [P, KD, F], F32R, at=nxt)
    wdT_hi, _, nxt = place("wdT_hi", [P, NF, D], F32R, at=nxt)
    wdT_lo, _, nxt = place("wdT_lo", [P, NF, D], F32R, at=nxt)
    assert nxt <= region_b + 4 * 8 * E
    assert mem["at"] <= nc.sbuf_usable_end, mem["at"] - nc.sbuf_usable_end

    banks = [nc.alloc_psum_tensor(f"bank{i}", [P, 512], F32) for i in range(8)]
    y_ps = banks[0:2]
    proj_ps = banks[2:4]
    s_ps = banks[4:6]
    t_ps = banks[6]
    o_ps = banks[7]
    one_ps = banks[2]
    pT_ps = (banks[3], banks[6])
    low_ps = banks[2]
    up_ps = banks[4:8]

    names = []

    def sem(name):
        names.append(name)
        return nc.alloc_semaphore(name)

    ld_x0, ld_xr, ld_wq, ld_wk, ld_wv, ld_wp, ld_b = (
        sem(n) for n in ("ld_x0", "ld_xr", "ld_wq", "ld_wk", "ld_wv", "ld_wp", "ld_b"))
    out_done = sem("out_done")
    ld_raw, ld_bhi, ld_bb = sem("ld_raw"), sem("ld_bhi"), sem("ld_bb")
    ld_ctx, ld_cw, ld_idx, ld_top = sem("ld_ctx"), sem("ld_cw"), sem("ld_idx"), sem("ld_top")
    wb_lo, g_tick = sem("wb_lo"), sem("g_tick")
    b_cT, b_chi, b_clo, b_blk, b_q, b_k, b_v = (
        sem(n) for n in ("b_cT", "b_chi", "b_clo", "b_blk", "b_q", "b_k", "b_v"))
    b_S, b_mx, b_nm, b_e, b_rs, b_p, b_T = (sem(n) for n in ("b_S", "b_mx", "b_nm", "b_e", "b_rs", "b_p", "b_T"))
    b_pT, b_av, b_ohi, b_olo, b_pj = (sem(n) for n in ("b_pT", "b_av", "b_ohi", "b_olo", "b_pj"))
    b_z, b_x = sem("b_z"), sem("b_x")
    g_lb, cw_T, cw_hi, cw_lo = sem("g_lb"), sem("cw_T"), sem("cw_hi"), sem("cw_lo")
    c_t, c_thi, c_tlo, c_u, c_u2 = (sem(n) for n in ("c_t", "c_thi", "c_tlo", "c_u", "c_u2"))
    c_g0, c_r1, c_g, c_ghi, c_glo, c_dn, c_x = (sem(n) for n in ("c_g0", "c_r1", "c_g", "c_ghi", "c_glo", "c_dn", "c_x"))
    g_const, g_rstd = sem("g_const"), sem("g_rstd")
    w_T, w_hi, w_lo = sem("w_T"), sem("w_hi"), sem("w_lo")
    idb = sem("idb")
    ln_bn, ln_mv, ln_xn, ln_T, ln_hi, ln_lo = (sem(n) for n in ("ln_bn", "ln_mv", "ln_xn", "ln_T", "ln_hi", "ln_lo"))
    g_veps = sem("g_veps")
    a_blk, a_sgn, a_ri, a_fx = sem("a_blk"), sem("a_sgn"), sem("a_ri"), sem("a_fx")
    a_S, a_y, a_near, a_si, a_clip, a_e = (sem(n) for n in ("a_S", "a_y", "a_near", "a_si", "a_clip", "a_e"))
    a_rs, a_rsc, a_p, a_T, a_aT = (sem(n) for n in ("a_rs", "a_rsc", "a_p", "a_T", "a_aT"))
    a_av, a_onear, a_oi, a_ohi, a_olo, a_pj = (sem(n) for n in ("a_av", "a_onear", "a_oi", "a_ohi", "a_olo", "a_pj"))
    a_z, a_zn, a_zi, a_zf, a_x = (sem(n) for n in ("a_z", "a_zn", "a_zi", "a_zf", "a_x"))

    def wait(eng, s, value):
        if isinstance(value, int) and value <= 0:
            return
        eng.wait_ge(s, value)

    PREP = []
    for sec in range(3):
        for half in range(2):
            for kt in range(KD):
                PREP.append(("qkv", sec * 8 + half * 4, kt))
    for et in range(0, NP, 2):
        PREP.append(("proj", et, None))

    B_CHUNKS = [(Wq.rearrange("(t p) e -> p t e", p=P)[:, i, :], wq_hi[:, i, :], wq_lo[:, i, :]) for i in range(KD)]
    B_CHUNKS += [(Wk, wk_hi[:, :], wk_lo[:, :]), (Wv, wv_hi[:, :], wv_lo[:, :])]
    B_CHUNKS += [(Wo.rearrange("(t p) d -> p t d", p=P)[:, 4 * i:4 * i + 4, :], wo_hi[:, 4 * i:4 * i + 4, :],
                  wo_lo[:, 4 * i:4 * i + 4, :]) for i in range(2)]

    C_PREP = [("la", 0, None)] + [("up", t, kt) for t in (0, 4) for kt in range(KD)]
    C_PREP += [("lb1", t, None) for t in (0, 4)] + [("lb2", t, None) for t in (0, 4)]
    C_PREP += [("down", t, None) for t in range(0, NF, 2)]
    C_BANKS = [banks[(2, 4, 5)[n % 3] if n < 9 else (6, 7, 3, 6)[n - 9]] for n in range(len(C_PREP))]
    C_PARTS = [range(0, 6), range(6, 9), range(9, len(C_PREP))]

    with nc.Block() as block:

        @block.sync
        def _(sp):
            sp.dma_start(x_sb[:, 0:GB, :], x[0:GB].rearrange("b p d -> p b d")).then_inc(ld_x0, 16)
            rows = w_qkv.rearrange("(t p) d -> p t d", p=P)
            for i, s_ in enumerate((ld_wq, ld_wk, ld_wv)):
                sp.dma_start(wqkv_raw[:, 8 * i:8 * i + 8, :], rows[:, 8 * i:8 * i + 8, :]).then_inc(s_, 16)
            sp.dma_start(wp_raw[:, :, :], w_proj.rearrange("(t p) e -> p t e", p=P)).then_inc(ld_wp, 16)
            for g in range(1, G):
                sp.dma_start(x_sb[:, g * GB:(g + 1) * GB, :],
                             x[g * GB:(g + 1) * GB].rearrange("b p d -> p b d")).then_inc(ld_xr, 16)
            sp.dma_start(bias_a[:, :], b_proj.partition_broadcast(P)).then_inc(ld_b, 16)
            sp.dma_start(bias_b[:, :], bo.partition_broadcast(P)).then_inc(ld_bb, 16)
            sp.dma_start(top_sb[:, :], top_v.partition_broadcast(P)).then_inc(ld_top, 16)
            sp.wait_ge(w_lo, len(PREP))
            for n, (src, hi, lo) in enumerate(B_CHUNKS):
                wait(sp, wb_lo, n)
                dst = raw_b[:, :] if len(src.shape) == 2 else raw_b[:, :].rearrange("p (a d) -> p a d", d=src.shape[2])
                sp.dma_start(dst, src).then_inc(ld_raw, 16)
            sp.wait_ge(a_blk, BLOCKS * G)
            sp.dma_start(idx_sb[:, :], top_i.rearrange("(a k) -> a k", a=1)).then_inc(ld_idx, 16)
            for g in range(G):
                wait(sp, b_cT, g)
                sp.dma_start(ctx_sb[:, :, :], ctx[g * GB:(g + 1) * GB].rearrange("b p d -> p b d")).then_inc(ld_ctx, 16)
                if g == 0:
                    sp.dma_start(wi_raw[:, :, :], wi_w.rearrange("(t p) d -> p t d", p=P)).then_inc(ld_cw, 16)
                    sp.dma_start(wd_raw[:, :, :], wo_w.rearrange("(t p) f -> p t f", p=P)).then_inc(ld_cw, 16)
                    sp.wait_ge(ld_idx, 16)
                    for k in range(2):
                        expert = sp.value_load(idx_sb[0:1, k:k + 1], min_val=0, max_val=lora_As.shape[0] - 1)
                        sp.dma_start(la_raw[k * RANK:(k + 1) * RANK, :],
                                     lora_As[bass.ds(expert, 1), :, :].rearrange("a r d -> (a r) d")).then_inc(ld_cw, 16)
                        sp.dma_start(lb_raw[:, :, k, :],
                                     lora_Bs[bass.ds(expert, 1), :, :].rearrange("a (t p) r -> p (a t) r", p=P)).then_inc(ld_cw, 16)
            for g in range(G):
                sp.wait_ge(c_x, 2 * g + 2)
                sp.dma_start(out[g * GB:(g + 1) * GB].rearrange("b p d -> p b d"),
                             x_sb[:, g * GB:(g + 1) * GB, :]).then_inc(out_done, 16)
            sp.wait_ge(out_done, 16 * G)

        @block.gpsimd
        def _(pool):
            nc.gpsimd.memset(ident[:, :], 0.0).then_inc(g_const, 1)
            nc.gpsimd.memset(mhalf[:, :], -0.5).then_inc(g_const, 1)
            nc.gpsimd.memset(growth[:, :], FIX * GROW).then_inc(g_const, 1)
            pool.wait_ge(g_const, 3)
            nc.gpsimd.affine_select(out=ident[:, :], in_=ident[:, :], compare_op=ALU.not_equal, fill=1.0,
                                    base=0, pattern=[[-1, P]], channel_multiplier=1).then_inc(g_const, 1)

            def inv_std(n):
                wait(pool, ln_mv, n + 1)
                nc.gpsimd.sem_inc(g_tick, 1)
                nc.gpsimd.tensor_scalar(veps[:, :], mv[:, :, 1], EPS, None, ALU.add).then_inc(g_veps, 1)
                wait(pool, g_veps, n + 1)
                nc.gpsimd.tensor_tensor(rstd[:, :], veps[:, :], mhalf[:, :], ALU.pow).then_inc(g_rstd, 1)

            def a_weights(n):
                wait(pool, a_rs, n + 1)
                nc.gpsimd.tensor_tensor(rsc[:, :], rsum[:, :], growth[:, :], ALU.mult).then_inc(a_rsc, 1)
                wait(pool, a_T, n)
                wait(pool, a_rsc, n + 1)
                nc.gpsimd.sem_inc(g_tick, 1)
                for t in range(8):
                    i = nc.gpsimd.tensor_scalar(p_int[:, t, :], e_sb[:, t, :], rsc[:, t:t + 1], -0.5,
                                                ALU.mult, ALU.add)
                i.then_inc(a_p, 1)

            def a_slot(g, s, first=False):
                if not (first and s == 0):
                    a_weights(NP * g + s - 1)
                if s == 2:
                    inv_std(g + 1)

            inv_std(0)
            pool.wait_ge(w_lo, len(PREP))
            for src, hi, lo in B_CHUNKS:
                nc.gpsimd.dma_start(hi, src).then_inc(ld_bhi, 16)
            for s in range(NP):
                a_slot(0, s, first=True)
                if s == 1:
                    pool.wait_ge(ld_bhi, 16 * len(B_CHUNKS))
                if 1 <= s < 1 + len(B_CHUNKS):
                    _, hi, lo = B_CHUNKS[s - 1]
                    raw = raw_b[:, :] if len(hi.shape) == 2 else raw_b[:, :].rearrange("p (a d) -> p a d", d=hi.shape[2])
                    pool.wait_ge(ld_raw, 16 * s)
                    nc.gpsimd.tensor_tensor(lo, raw, hi.bitcast(F32), ALU.subtract).then_inc(wb_lo, 1)
            with pool.Fori(1, G) as g:
                for s in range(NP):
                    a_slot(g, s)
            a_weights(NP * G - 1)

            def b_weights(n):
                wait(pool, b_rs, n + 1)
                wait(pool, b_T, n)
                nc.gpsimd.sem_inc(g_tick, 1)
                for t in range(8):
                    i = nc.gpsimd.tensor_scalar(p_f[:, t, :], e_sb[:, t, :], rsum[:, t:t + 1], 0.0, ALU.mult, ALU.add)
                i.then_inc(b_p, 1)

            def b_slot(g, s, first=False):
                if not (first and s == 0):
                    b_weights(NP * g + s - 1)
                if s == 4:
                    inv_std(G + g + 1)

            for s in range(NP):
                b_slot(0, s, first=True)
                if s == 1:
                    pool.wait_ge(ld_cw, 16 * 6)
                    nc.gpsimd.memset(lb1[:, :, :, 1, :], 0.0).then_inc(g_lb, 1)
                    for j in range(3):
                        nc.gpsimd.tensor_copy(lb1[:, :, j, 0, :], lb_raw[:, :, 0, :]).then_inc(g_lb, 1)
                        nc.gpsimd.tensor_scalar(lb2[:, :, j, 0, :], lb_raw[:, :, 0, :], -1.0, 0.0, ALU.mult,
                                                ALU.add).then_inc(g_lb, 1)
                        nc.gpsimd.tensor_copy(lb2[:, :, j, 1, :], lb_raw[:, :, 1, :]).then_inc(g_lb, 1)
            with pool.Fori(1, G) as g:
                for s in range(NP):
                    b_slot(g, s)
            b_weights(NP * G - 1)
            for g in range(G):
                inv_std(2 * G + g + 1)

        @block.tensor
        def _(pe):
            def split3(out_, w_pair, m_pair, first, last, **kw):
                (wh, wl), (mh, ml) = w_pair, m_pair
                pe.matmul(out_, wl, mh, start=first, stop=False, **kw)
                pe.matmul(out_, wh, ml, start=False, stop=False, **kw)
                return pe.matmul(out_, wh, mh, start=False, stop=last, **kw)

            pe.wait_ge(g_const, 4)
            for n, (what, t, kt) in enumerate(PREP):
                if what == "qkv":
                    if t % 8 == 0 and kt == 0:
                        pe.wait_ge((ld_wq, ld_wk, ld_wv)[t // 8], 16)
                elif t == 0:
                    pe.wait_ge(ld_wp, 16)
                wait(pe, w_lo, n - 7)
                for j in range(4):
                    if what == "qkv":
                        src = wqkv_raw[:, t + j, kt * P:(kt + 1) * P]
                    else:
                        src = wp_raw[:, j % 2, (t + j // 2) * P:(t + j // 2 + 1) * P]
                    last = pe.transpose(banks[n % 8][:, j * P:(j + 1) * P], src, ident[:, :])
                last.then_inc(w_T, 1)
            pe.wait_ge(w_lo, len(PREP))
            pe.wait_ge(idb, 1)

            def normed_T(n, prev_reads):
                wait(pe, ln_xn, n + 1)
                prev_reads()
                for kt in range(KD):
                    for b in range(GB):
                        last = pe.transpose(proj_ps[kt][:, b * P:(b + 1) * P], xn[:, b, kt * P:(kt + 1) * P],
                                            ident[:, :])
                    last.then_inc(ln_T, 1)

            def a_block(g, m, w0, moving_tokens):
                if m < 2:
                    wait(pe, ln_lo, 2 * g + 2)
                else:
                    wait(pe, a_ri, BLOCKS * g + m - 1)
                ps = proj_ps[m % 2]
                for kt in range(KD):
                    if moving_tokens:
                        wp = [w[:, kt, w0:w0 + P] for w in (wqkvT_hi, wqkvT_lo)]
                        mp = [t[:, kt, :] for t in (xnT_hi, xnT_lo)]
                    else:
                        b, col = w0
                        wp = [t[:, kt, b * P:(b + 1) * P] for t in (xnT_hi, xnT_lo)]
                        mp = [w[:, kt, col:col + 512] for w in (wqkvT_hi, wqkvT_lo)]
                    last = split3(ps[:, :], wp, mp, kt == 0, kt == KD - 1)
                last.then_inc(a_blk, 1)

            def a_transpose(n):
                wait(pe, a_p, n + 1)
                wait(pe, a_aT, n)
                for t in range(8):
                    last = pe.transpose(t_ps[:, t * 64:(t + 1) * 64].bitcast(BF16),
                                        p_int[:, t, :].bitcast(BF16), ident_b[:, :])
                last.then_inc(a_T, 1)

            def a_attend(n, p, v_count):
                wait(pe, a_aT, n + 1)
                wait(pe, a_fx, v_count)
                wait(pe, a_oi, n)
                for b in range(GB):
                    for hh in range(2):
                        h0 = (2 * p + hh) * DH
                        last = pe.matmul(o_ps[hh * DH:(hh + 1) * DH, b * P:(b + 1) * P], v_sb[:, b, h0:h0 + DH],
                                         aT_sb[:, GB * hh + b, :], start=True, stop=True)
                last.then_inc(a_av, 1)

            def project_out(n, p, ready, done, weights, y_free):
                wait(pe, ready, n + 1)
                if p == 0:
                    wait(pe, *y_free)
                for b in range(GB):
                    first = p == 0 and b % 2 == 0
                    last = split3(y_ps[b // 2][:, (b % 2) * D:(b % 2 + 1) * D],
                                  [t[:, b * P:(b + 1) * P] for t in (oT_hi, oT_lo)],
                                  [w[:, p, :] for w in weights], first, p == NP - 1, skip_group_check=True)
                last.then_inc(done, 1)

            def a_scores(n, s, blk):
                wait(pe, a_fx, blk)
                wait(pe, a_y, 2 * n)
                for b in range(GB):
                    for hh in range(2):
                        last = pe.matmul(s_ps[hh][:, b * P:(b + 1) * P],
                                         q_sb[hh * DH:(hh + 1) * DH, s % 2, b * P:(b + 1) * P],
                                         k_sb[hh * DH:(hh + 1) * DH, s % 2, b * P:(b + 1) * P],
                                         start=True, stop=True)
                        if b == GB - 1:
                            last.then_inc(a_S, 1)

            def a_slot(g, s, first=False, drain=False):
                n = NP * g + s
                base = block_index(s)
                if s > 0 and not drain:
                    a_block(g, base, s * P, True)
                    a_block(g, base + 1, E + s * P, True)
                lag2 = not (first and s < 2) and not (drain and s >= 2)
                if lag2 and (s > 0 or drain):
                    a_transpose(n - 2)
                if not (first and s < 3):
                    p = (s - 3) % NP
                    project_out(n - 3, p, a_olo, a_pj, (wpT_hi, wpT_lo), (a_z, 2 * g))
                if s == 0 and not drain:
                    a_block(g, base, s * P, True)
                    if lag2:
                        a_transpose(n - 2)
                    a_block(g, base + 1, E + s * P, True)
                if lag2:
                    p = (s - 2) % NP
                    gg = g if s >= 2 else g - 1
                    a_attend(n - 2, p, BLOCKS * gg + (block_index(1) + 4 if p < 4 else block_index(3) + 4))
                if s < 4 and not drain:
                    for i in range(2):
                        j = 2 * s + i
                        a_block(g, base + 2 + i, (j % 4, 2 * E + 512 * (j // 4)), False)
                if s == NP - 1:
                    normed_T(g + 1, lambda: wait(pe, a_ri, BLOCKS * (g + 1)))
                if not drain:
                    a_scores(n, s, BLOCKS * g + base + 2)

            normed_T(0, lambda: None)
            for s in range(NP):
                a_slot(0, s, first=True)
            with pe.Fori(1, G) as g:
                for s in range(NP):
                    a_slot(g, s)

            pe.wait_ge(wb_lo, len(B_CHUNKS))

            def b_block(g, s, what, i=0):
                if what == "q":
                    wait(pe, ln_lo, 2 * (G + g) + 2)
                    if s == 0:
                        wait(pe, b_clo, g + 1)
                    elif s <= 4:
                        wait(pe, b_v, 8 * g + 2 * s)
                    else:
                        wait(pe, b_k, NP * g + s)
                    for kt in range(KD):
                        last = split3(one_ps[:, :], [w[:, kt, s * P:(s + 1) * P] for w in (wq_hi, wq_lo)],
                                      [t[:, kt, :] for t in (xnT_hi, xnT_lo)], kt == 0, kt == KD - 1)
                elif what == "k":
                    if s < 4:
                        wait(pe, b_v, 8 * g + 2 * s + 1)
                    else:
                        wait(pe, b_q, NP * g + s + 1)
                    last = split3(one_ps[:, :], [w[:, s * P:(s + 1) * P] for w in (wk_hi, wk_lo)],
                                  [t[:, :] for t in (cT_hi, cT_lo)], True, True)
                else:
                    if i == 0:
                        wait(pe, b_q, NP * g + s + 1)
                    else:
                        wait(pe, b_k, NP * g + s + 1)
                    b, col = (2 * s + i) % 4, 512 * ((2 * s + i) // 4)
                    last = split3(one_ps[:, :], [t[:, b * P:(b + 1) * P] for t in (cT_hi, cT_lo)],
                                  [w[:, col:col + 512] for w in (wv_hi, wv_lo)], True, True)
                last.then_inc(b_blk, 1)

            def b_transpose(n):
                wait(pe, b_p, n + 1)
                if isinstance(n, int) and n == 0:
                    wait(pe, a_aT, NP * G)
                wait(pe, b_pT, n)
                for hh in range(2):
                    for b in range(GB):
                        last = pe.transpose(pT_ps[hh][:, b * P:(b + 1) * P], p_f[:, GB * hh + b, :], ident[:, :])
                last.then_inc(b_T, 1)

            def b_attend(n, p, v_count):
                wait(pe, b_pT, n + 1)
                wait(pe, b_v, v_count)
                if isinstance(n, int) and n == 0:
                    wait(pe, a_oi, NP * G)
                wait(pe, b_olo, n)
                for b in range(GB):
                    for hh in range(2):
                        h0 = (2 * p + hh) * DH
                        last = pe.matmul(o_ps[hh * DH:(hh + 1) * DH, b * P:(b + 1) * P], v_sb[:, b, h0:h0 + DH],
                                         aT_sb[:, GB * hh + b, :], start=True, stop=True)
                last.then_inc(b_av, 1)

            def b_scores(g, n, s):
                wait(pe, b_q, n + 1)
                wait(pe, b_k, n + 1)
                if isinstance(n, int) and n == 0:
                    wait(pe, a_y, 2 * NP * G)
                wait(pe, b_e, n)
                for b in range(GB):
                    for hh in range(2):
                        last = pe.matmul(s_ps[hh][:, b * P:(b + 1) * P],
                                         q_sb[hh * DH:(hh + 1) * DH, s % 2, b * P:(b + 1) * P],
                                         k_sb[hh * DH:(hh + 1) * DH, s % 2, b * P:(b + 1) * P],
                                         start=True, stop=True)
                        if b == GB - 1:
                            last.then_inc(b_S, 1)

            def b_slot(g, s, first=False, drain=False):
                n = NP * g + s
                lag2 = not (first and s < 2) and not (drain and s >= 2)
                if s == 0 and not drain:
                    wait(pe, ld_ctx, 16 * (g + 1))
                    wait(pe, ln_lo, 2 * (G + g) + 1)
                    for b in range(GB):
                        last = pe.transpose(one_ps[:, b * P:(b + 1) * P], ctx_sb[:, b, :], ident[:, :])
                    last.then_inc(b_cT, 1)
                def transposes():
                    if first and s < 2:
                        a_transpose(NP * G + s - 2)
                    if lag2:
                        if s == 0:
                            wait(pe, ln_lo, 2 * (G + g) + 2)
                        b_transpose(n - 2)

                def project():
                    if first and s < 3:
                        project_out(NP * G + s - 3, NP + s - 3, a_olo, a_pj, (wpT_hi, wpT_lo), None)
                    else:
                        project_out(n - 3, (s - 3) % NP, b_olo, b_pj, (wo_hi, wo_lo),
                                    (a_z, 2 * G) if first else (b_z, 2 * g))

                def attend():
                    if first and s < 2:
                        a_attend(NP * G + s - 2, NP + s - 2, BLOCKS * (G - 1) + block_index(3) + 4)
                    if lag2:
                        p = (s - 2) % NP
                        gg = g if s >= 2 else g - 1
                        b_attend(n - 2, p, 8 * gg + (4 if p < 4 else 8))

                if drain:
                    transposes()
                    project()
                    attend()
                elif first and s == 0:
                    project()
                    b_block(g, s, "q")
                    transposes()
                    b_block(g, s, "v", 0)
                    attend()
                    b_block(g, s, "k")
                elif s == 0:
                    transposes()
                    b_block(g, s, "q")
                    project()
                    b_block(g, s, "v", 0)
                    attend()
                    b_block(g, s, "k")
                else:
                    b_block(g, s, "q")
                    transposes()
                    if s < 4:
                        b_block(g, s, "v", 0)
                    project()
                    b_block(g, s, "k")
                    attend()
                if not drain:
                    if s < 4:
                        b_block(g, s, "v", 1)
                    if s == NP - 1:
                        def free():
                            wait(pe, b_k, n + 1)
                            wait(pe, b_pT, n - 1)
                        normed_T(G + g + 1, free)
                    b_scores(g, n, s)

            for s in range(NP):
                b_slot(0, s, first=True)
            with pe.Fori(1, G) as g:
                for s in range(NP):
                    b_slot(g, s)
            def c_weights(part):
                for n in part:
                    what, t, kt = C_PREP[n]
                    wait(pe, cw_lo, n - 2 if n < 9 else 10 if n == 12 else 0)
                    for j in range(4):
                        if what == "up":
                            last = pe.transpose(C_BANKS[n][:, j * P:(j + 1) * P], wi_raw[:, t + j, kt * P:(kt + 1) * P],
                                                ident[:, :])
                        elif what == "down":
                            f0 = (t + j // 2) * P
                            last = pe.transpose(C_BANKS[n][:, j * P:(j + 1) * P], wd_raw[:, j % 2, f0:f0 + P], ident[:, :])
                        elif what in ("lb1", "lb2"):
                            src = (lb1 if what == "lb1" else lb2)[:, t + j, :, :, :].rearrange("p c k r -> p (c k r)")
                            last = pe.transpose(C_BANKS[n][0:96, j * P:(j + 1) * P], src, ident[:, :])
                        elif j < KD:
                            last = pe.transpose(C_BANKS[n][:, j * 32:(j + 1) * 32], la_raw[:, j * P:(j + 1) * P],
                                                ident[0:32, 0:32])
                    last.then_inc(cw_T, 1)

            for s in range(2):
                b_slot(G, s, drain=True)
                if s == 0:
                    pe.wait_ge(g_lb, 10)
                    pe.wait_ge(b_e, NP * G)
                c_weights(C_PARTS[s])
            pe.wait_ge(cw_lo, 9)

            def c_slot(g, s, first=False, drain=False):
                n = NF * g + s

                def up():
                    wait(pe, c_r1, n - 3)
                    u = up_ps[s % 4]
                    for kt in range(KD):
                        split3(u[:, :], [w[:, kt, s * P:(s + 1) * P] for w in (wiT_hi, wiT_lo)],
                               [t[:, kt, :] for t in (xnT_hi, xnT_lo)], kt == 0, False)
                    wait(pe, c_tlo, g + 1)
                    pe.matmul(u[:, :], lb1T[:, s * P:(s + 1) * P], lowT[:, :], start=False, stop=True).then_inc(c_u, 1)

                if first and s == 2:
                    wait(pe, cw_lo, len(C_PREP))
                if not drain and s > 0:
                    up()
                if s == NF - 1:
                    normed_T(2 * G + g + 1, lambda: wait(pe, c_tlo, g + 1))
                if not (first and s < 1) and not (drain and s >= 1):
                    p = (s - 1) % NF
                    wait(pe, c_g0, n)
                    pe.matmul(up_ps[p % 4][:, :], lb2T[:, p * P:(p + 1) * P], lowT[:, :], start=False, stop=True,
                              skip_group_check=True).then_inc(c_u2, 1)
                if not (first and s < 3):
                    p = (s - 3) % NF
                    wait(pe, c_glo, n - 2)
                    if p == 0 and first:
                        wait(pe, b_z, 2 * G)
                    elif p == 0:
                        wait(pe, c_x, 2 * g)
                    for b in range(GB):
                        last = split3(y_ps[b // 2][:, (b % 2) * D:(b % 2 + 1) * D],
                                      [t[p % 2][:, b * P:(b + 1) * P] for t in (tile_hi, tile_lo)],
                                      [w[:, p, :] for w in (wdT_hi, wdT_lo)], p == 0 and b % 2 == 0, p == NF - 1,
                                      skip_group_check=True)
                    last.then_inc(c_dn, 1)
                if s == 0 and not drain:
                    wait(pe, ln_lo, 2 * (2 * G + g) + 2)
                    for kt in range(KD):
                        last = split3(low_ps[:, :], [w[:, kt, :] for w in (laT_hi, laT_lo)],
                                      [t[:, kt, :] for t in (xnT_hi, xnT_lo)], kt == 0, kt == KD - 1)
                    last.then_inc(c_t, 1)
                    if first:
                        b_slot(G, 2, drain=True)
                        pe.wait_ge(b_pT, NP * G)
                        pe.wait_ge(b_olo, NP * G)
                        c_weights(C_PARTS[2])
                    up()

            for s in range(NF):
                c_slot(0, s, first=True)
            with pe.Fori(1, G) as g:
                for s in range(NF):
                    c_slot(g, s)
            for s in range(3):
                c_slot(G, s, drain=True)

        @block.scalar
        def _(act):
            for n, (what, t, kt) in enumerate(PREP):
                act.wait_ge(w_T, n + 1)
                dst = wqkvT_hi[:, kt, t * P:t * P + 512] if what == "qkv" else wpT_hi[:, t:t + 2, :].rearrange("p a d -> p (a d)")
                nc.scalar.activation(dst, banks[n % 8][:, :], ACT.Copy,
                                     scale=FIX * GROW if what == "qkv" else 1.0).then_inc(w_hi, 1)

            def xnT_high(n):
                for kt in range(KD):
                    wait(act, ln_T, 2 * n + kt + 1)
                    nc.scalar.copy(xnT_hi[:, kt, :], proj_ps[kt][:, :]).then_inc(ln_hi, 1)

            def sign_of(g, m):
                wait(act, a_blk, BLOCKS * g + m + 1)
                wait(act, a_ri, BLOCKS * g + m - 1)
                nc.scalar.activation(sgn[:, m % 2, :], proj_ps[m % 2][:, :], ACT.Sign).then_inc(a_sgn, 1)

            def a_weightsT(n):
                wait(act, a_T, n + 1)
                wait(act, a_av, n)
                nc.scalar.activation(aT_sb[:, :, :].rearrange("p a t -> p (a t)"), t_ps[:, :].bitcast(I16),
                                     ACT.Copy, scale=1.0 / FIX).then_inc(a_aT, 1)

            def a_exp(n):
                wait(act, a_p, n)
                wait(act, a_rs, n)
                for i in range(2):
                    wait(act, a_clip, 2 * n + 1 + i)
                    for j in range(4):
                        t = 4 * i + j
                        last = nc.scalar.activation(e_sb[:, t, :], si[:, i, j * P:(j + 1) * P], ACT.Exp,
                                                    scale=1.0 / FIX, accum_out=sums[:, t:t + 1])
                    last.then_inc(a_e, 1)

            def a_high(n):
                wait(act, a_oi, n + 1)
                wait(act, a_pj, n)
                nc.scalar.copy(oT_hi[:, :], oi[:, :]).then_inc(a_ohi, 1)

            def a_slot(g, s, first=False, drain=False):
                n = NP * g + s
                base = block_index(s)
                if not drain:
                    if s > 0:
                        sign_of(g, base)
                        sign_of(g, base + 1)
                lag2 = not (first and s < 2)
                if lag2:
                    a_weightsT(n - 2)
                if not drain and s == 0:
                    sign_of(g, base)
                    sign_of(g, base + 1)
                if not (first and s == 0):
                    a_exp(n - 1)
                if not drain:
                    if s < 4:
                        sign_of(g, base + 2)
                        sign_of(g, base + 3)
                if lag2:
                    a_high(n - 2)
                if not drain:
                    if s == NP - 1:
                        xnT_high(g + 1)
                    for i in range(2):
                        wait(act, a_S, 2 * n + i + 1)
                        wait(act, a_si, 2 * n + i - 1)
                        nc.scalar.copy(y_sb[:, i, :], s_ps[i][:, :]).then_inc(a_y, 1)

            xnT_high(0)
            for s in range(NP):
                a_slot(0, s, first=True)
            with act.Fori(1, G) as g:
                for s in range(NP):
                    a_slot(g, s)

            def b_slot(g, s, first=False, drain=False):
                n = NP * g + s
                lag2 = not (first and s < 2) and not (drain and s >= 2)
                if not drain:
                    if s == 0:
                        wait(act, b_cT, g + 1)
                        nc.scalar.copy(cT_hi[:, :], one_ps[:, :]).then_inc(b_chi, 1)
                    wait(act, b_S, 2 * n - 2)
                    wait(act, b_blk, BLOCKS * g + block_index(s) + 1)
                    if first and s < 2:
                        wait(act, a_S, 2 * (NP * G + s) - 2)
                    nc.scalar.copy(q_sb[:, s % 2, :], one_ps[:, :]).then_inc(b_q, 1)
                if first and s < 2:
                    a_weightsT(NP * G + s - 2)
                if first and s == 0:
                    a_exp(NP * G - 1)
                if (not (first and s == 0)) and not (drain and s >= 1):
                    if first and s == 1:
                        wait(act, a_p, NP * G)
                    wait(act, b_p, n - 1)
                    wait(act, b_rs, n - 1)
                    for hh in range(2):
                        wait(act, b_nm, 2 * n - 1 + hh)
                        for t in range(GB * hh, GB * hh + GB):
                            last = nc.scalar.activation(e_sb[:, t, :], s_ps[hh][:, (t % 4) * P:(t % 4 + 1) * P], ACT.Exp,
                                                        bias=neg_max[:, t:t + 1], scale=DH ** -0.5,
                                                        accum_out=sums[:, t:t + 1])
                    last.then_inc(b_e, 1)
                if first and s < 2:
                    a_high(NP * G + s - 2)
                if lag2:
                    wait(act, b_av, n - 1)
                    if first and s == 2:
                        wait(act, a_pj, NP * G)
                    wait(act, b_pj, n - 2)
                    nc.scalar.copy(oT_hi[:, :], o_ps[:, :]).then_inc(b_ohi, 1)
                if s == NP - 1:
                    xnT_high(G + g + 1)

            for s in range(NP):
                b_slot(0, s, first=True)
            with act.Fori(1, G) as g:
                for s in range(NP):
                    b_slot(g, s)
            def c_weights(part):
                for n in part:
                    what, t, kt = C_PREP[n]
                    act.wait_ge(cw_T, n + 1)
                    bank = C_BANKS[n]
                    if what == "up":
                        last = nc.scalar.copy(wiT_hi[:, kt, t * P:t * P + 512], bank[:, :])
                    elif what == "down":
                        last = nc.scalar.copy(wdT_hi[:, t:t + 2, :].rearrange("p a d -> p (a d)"), bank[:, :])
                    elif what in ("lb1", "lb2"):
                        last = nc.scalar.copy((lb1T if what == "lb1" else lb2T)[:, t * P:t * P + 512], bank[0:96, :])
                    else:
                        for j in range(4):
                            last = nc.scalar.copy(laT_hi[:, :, 32 * j:32 * j + 32],
                                                  bank[:, 0:64].rearrange("p (k r) -> p k r", k=KD))
                    last.then_inc(cw_hi, 1)

            for s in range(2):
                b_slot(G, s, drain=True)
                c_weights(C_PARTS[s])

            def c_slot(g, s, first=False, drain=False):
                n = NF * g + s
                if s == NF - 1:
                    xnT_high(2 * G + g + 1)
                if not (first and s < 1) and not (drain and s >= 1):
                    p = (s - 1) % NF
                    wait(act, c_u2, n)
                    wait(act, c_g, n - 1)
                    nc.scalar.activation(relu1[:, :], up_ps[p % 4][:, :], ACT.Relu).then_inc(c_r1, 1)
                    wait(act, c_g, n)
                    if first and s == 1:
                        wait(act, b_pj, NP * G)
                    wait(act, c_dn, n - 2)
                    nc.scalar.copy(tile_hi[p % 2][:, :], hid[:, :]).then_inc(c_ghi, 1)
                if s == 0 and not drain:
                    wait(act, c_t, g + 1)
                    nc.scalar.copy(lowT[:, :], low_ps[0:96, :]).then_inc(c_thi, 1)
                    if first:
                        c_weights(C_PARTS[2])

            for s in range(NF):
                c_slot(0, s, first=True)
            with act.Fori(1, G) as g:
                for s in range(NF):
                    c_slot(g, s)
            c_slot(G, 0, drain=True)

        @block.vector
        def _(dve):
            V = nc.vector

            def norm_stats(n, g, batches=range(GB)):
                for b in batches:
                    i = V.bn_stats(bn_st[:, b, :], x_sb[:, bass.ds(g * GB + b, 1), :].rearrange("p a d -> p (a d)"))
                if GB - 1 in batches:
                    i.then_inc(ln_bn, 1)

            def add_rows(gp, j, z, done):
                xx = x_sb[:, bass.ds(gp * GB + 2 * j, 2), :].rearrange("p a d -> p (a d)")
                V.tensor_tensor(xx, xx, z, ALU.add).then_inc(done, 1)

            def norm_moments():
                for b in range(GB):
                    i = V.bn_aggr(mv[:, b, :], bn_st[:, b, :])
                i.then_inc(ln_mv, 1)

            def norm_apply(n, g, T_count, batches=range(GB)):
                wait(dve, T_count[0], T_count[1])
                wait(dve, g_rstd, n + 1)
                for b in batches:
                    i = V.tensor_scalar(xn[:, b, :], x_sb[:, bass.ds(g * GB + b, 1), :].rearrange("p a d -> p (a d)"),
                                        mv[:, b, 0:1], rstd[:, b:b + 1], ALU.subtract, ALU.mult)
                if GB - 1 in batches:
                    i.then_inc(ln_xn, 1)

            dve.wait_ge(ld_x0, 16)
            norm_stats(0, 0)
            dve.wait_ge(ln_bn, 1)
            norm_moments()
            norm_apply(0, 0, (ln_T, 0))
            dve.wait_ge(g_const, 4)
            V.tensor_copy(ident_b[:, :], ident[:, :]).then_inc(idb, 1)
            for n, (what, t, kt) in enumerate(PREP):
                dve.wait_ge(w_hi, n + 1)
                if what == "qkv":
                    hi, lo = (w[:, kt, t * P:t * P + 512] for w in (wqkvT_hi, wqkvT_lo))
                else:
                    hi, lo = (w[:, t:t + 2, :].rearrange("p a d -> p (a d)") for w in (wpT_hi, wpT_lo))
                V.scalar_tensor_tensor(lo, banks[n % 8][:, :], FIX * GROW if what == "qkv" else 1.0,
                                       hi.bitcast(F32), ALU.mult, ALU.subtract).then_inc(w_lo, 1)
            dve.wait_ge(ld_b, 16)
            dve.wait_ge(ld_xr, 48)
            V.tensor_scalar(bias_a[:, :], bias_a[:, :], FIX, None, ALU.mult).then_inc(idb, 1)

            def xnT_low(n):
                for kt in range(KD):
                    wait(dve, ln_hi, 2 * n + kt + 1)
                    V.tensor_tensor(xnT_lo[:, kt, :], proj_ps[kt][:, :], xnT_hi[:, kt, :].bitcast(F32),
                                    ALU.subtract).then_inc(ln_lo, 1)

            def fix_blocks(g, m, dsts, scales):
                for i in range(2):
                    wait(dve, a_sgn, BLOCKS * g + m + i + 1)
                    wait(dve, a_fx, BLOCKS * g + m + i - 1)
                    V.scalar_tensor_tensor(ri[:, i, :], sgn[:, i, :], -0.5, proj_ps[i][:, :],
                                           ALU.mult, ALU.add).then_inc(a_ri, 1)
                for i in range(2):
                    wait(dve, a_ri, BLOCKS * g + m + i + 1)
                    V.tensor_scalar(dsts[i], ri[:, i, :], LOW, scales[i], ALU.max, ALU.mult).then_inc(a_fx, 1)

            def qk(g, s, n):
                wait(dve, a_S, 2 * n - 2)
                m = block_index(s)
                fix_blocks(g, m, (q_sb[:, s % 2, :], k_sb[:, s % 2, :]), (1.0 / (FIX * DH ** 0.5), 1.0))

            def a_out(n):
                wait(dve, a_av, n + 1)
                V.tensor_scalar(near0[:, 0, :], o_ps[:, :], 0.5, -0.5, ALU.min, ALU.max).then_inc(a_onear, 1)
                wait(dve, a_onear, n + 1)
                V.scalar_tensor_tensor(oi[:, :], o_ps[:, :], GROW, near0[:, 0, :], ALU.mult,
                                       ALU.subtract).then_inc(a_oi, 1)

            def a_recip(n):
                wait(dve, a_e, 2 * n + 2)
                wait(dve, a_p, n)
                V.reciprocal(rsum[:, :], sums[:, :]).then_inc(a_rs, 1)

            def a_low(n):
                wait(dve, a_ohi, n + 1)
                V.tensor_tensor(oT_lo[:, :], oi[:, :], oT_hi[:, :].bitcast(F32), ALU.subtract).then_inc(a_olo, 1)

            def y_out(g):
                wait(dve, a_pj, NP * g)
                dve.wait_ge(wb_lo, len(B_CHUNKS))
                bias = bias_a[:, :].rearrange("p (a d) -> p a d", a=1).broadcast_to([P, 2, D])
                for j in range(2):
                    V.tensor_tensor(raw_b[:, j * TOK:(j + 1) * TOK].rearrange("p (a d) -> p a d", a=2),
                                    y_ps[j][:, :].rearrange("p (a d) -> p a d", a=2), bias, ALU.add).then_inc(a_z, 1)

            def fix_y(g, j, part):
                z, near = raw_b[:, j * TOK:(j + 1) * TOK], near0[:, j, :]
                count = 2 * (g - 1) + j + 1
                if part == 0:
                    wait(dve, a_z, count)
                    V.tensor_scalar(near, z, 0.5, -0.5, ALU.min, ALU.max).then_inc(a_zn, 1)
                    wait(dve, a_zn, count)
                    wait(dve, a_zf, count - 1)
                    V.scalar_tensor_tensor(zi[:, :], z, GROW, near, ALU.mult, ALU.subtract).then_inc(a_zi, 1)
                else:
                    wait(dve, a_zi, count)
                    V.tensor_scalar(z, zi[:, :], LOW, 1.0 / FIX, ALU.max, ALU.mult).then_inc(a_zf, 1)
                    wait(dve, a_zf, count)
                    if j == 1:
                        wait(dve, a_x, 2 * g - 1)
                    add_rows(g - 1, j, z, a_x)

            def between_groups(g, s, first, drain):
                if s == 1 and not drain:
                    norm_stats(g + 1, (g + 1) % G)
                if s == 2 and not drain:
                    norm_moments()
                if not first:
                    for slot, j, part in ((3, 0, 0), (4, 0, 1), (6, 1, 0), (7, 1, 1)):
                        if s == slot or drain and s == 2:
                            fix_y(g, j, part)
                if s in (3, 5) and not drain:
                    norm_apply(g + 1, (g + 1) % G, (ln_T, 2 * g + 2), (0, 1) if s == 3 else (2, 3))

            def a_slot(g, s, first=False, drain=False):
                n = NP * g + s
                base = block_index(s)
                lag2 = not (first and s < 2) and not (drain and s >= 2)
                if not drain:
                    if s == 2:
                        wait(dve, ln_bn, g + 2)
                    qk(g, s, n)
                if lag2:
                    a_out(n - 2)
                if not (first and s == 0):
                    a_recip(n - 1)
                if not drain and s < 4:
                    if s == 0 and not first:
                        wait(dve, a_av, NP * g - 4)
                    if s == 2:
                        wait(dve, a_av, NP * g)
                    fix_blocks(g, base + 2, [v_sb[:, j % 4, 512 * (j // 4):512 * (j // 4) + 512]
                                             for j in (2 * s, 2 * s + 1)], (1.0, 1.0))
                if s == 2 and not first:
                    y_out(g)
                if lag2:
                    a_low(n - 2)
                if s == NP - 1:
                    xnT_low(g + 1)
                if not drain:
                    for i in range(2):
                        wait(dve, a_y, 2 * n + i + 1)
                        V.tensor_scalar(near0[:, i, :], y_sb[:, i, :], 0.5, -0.5, ALU.min, ALU.max).then_inc(a_near, 1)
                    for i in range(2):
                        wait(dve, a_near, 2 * n + i + 1)
                        V.scalar_tensor_tensor(si[:, i, :], y_sb[:, i, :], GROW, near0[:, i, :], ALU.mult,
                                               ALU.subtract).then_inc(a_si, 1)
                    for i in range(2):
                        wait(dve, a_si, 2 * n + i + 1)
                        V.tensor_scalar(si[:, i, :], si[:, i, :], LOW, None, ALU.max).then_inc(a_clip, 1)
                between_groups(g, s, first, drain)

            xnT_low(0)
            for s in range(NP):
                a_slot(0, s, first=True)
            with dve.Fori(1, G) as g:
                for s in range(NP):
                    a_slot(g, s)

            dve.wait_ge(ld_bb, 16)

            def b_v_rows(g, s, i):
                j = 2 * s + i
                wait(dve, b_blk, BLOCKS * g + block_index(s) + 2 + 2 * i)
                V.tensor_copy(v_sb[:, j % 4, 512 * (j // 4):512 * (j // 4) + 512], one_ps[:, :]).then_inc(b_v, 1)

            def b_k_rows(g, s):
                n = NP * g + s
                if isinstance(n, int) and n < 2:
                    wait(dve, a_S, 2 * (NP * G + s) - 2)
                wait(dve, b_S, 2 * n - 2)
                wait(dve, b_blk, BLOCKS * g + block_index(s) + (3 if s < 4 else 2))
                V.tensor_copy(k_sb[:, s % 2, :], one_ps[:, :]).then_inc(b_k, 1)

            def b_slot(g, s, first=False, drain=False):
                n = NP * g + s
                lag2 = not (first and s < 2) and not (drain and s >= 2)
                if not drain:
                    if s == 0:
                        wait(dve, b_chi, g + 1)
                        V.tensor_tensor(cT_lo[:, :], one_ps[:, :], cT_hi[:, :].bitcast(F32), ALU.subtract).then_inc(b_clo, 1)
                    if s == 4:
                        wait(dve, ln_bn, G + g + 2)
                if first:
                    for slot, j, part in ((3, 0, 0), (4, 0, 1), (5, 1, 0), (6, 1, 1)):
                        if s == slot:
                            fix_y(G, j, part)
                if (not (first and s == 0)) and not (drain and s >= 1):
                    for hh in range(2):
                        wait(dve, b_S, 2 * n - 1 + hh)
                        half = slice(GB * hh, GB * hh + GB)
                        V.reduce_max(mx[:, half], s_ps[hh][:, :].rearrange("p (a t) -> p a t", a=GB), AX).then_inc(b_mx, 1)
                    for hh in range(2):
                        half = slice(GB * hh, GB * hh + GB)
                        wait(dve, b_mx, 2 * n - 1 + hh)
                        V.tensor_scalar(neg_max[:, half], mx[:, half], -DH ** -0.5, None, ALU.mult).then_inc(b_nm, 1)
                if lag2:
                    wait(dve, b_T, n - 1)
                    if first and s == 2:
                        wait(dve, a_av, NP * G)
                    wait(dve, b_av, n - 2)
                    for hh in range(2):
                        i = V.tensor_copy(aT_sb[:, GB * hh:GB * hh + GB, :].rearrange("p a t -> p (a t)"),
                                          pT_ps[hh][:, :])
                    i.then_inc(b_pT, 1)
                if s == 4 and not drain:
                    norm_moments()

                if not drain:
                    av, count = (a_av, NP * G) if first else (b_av, NP * g)
                    if s == 0:
                        wait(dve, av, count - 4)
                    if s == 2:
                        wait(dve, av, count)
                    if s < 4:
                        b_v_rows(g, s, 0)
                    b_k_rows(g, s)
                if first and s < 2:
                    a_out(NP * G + s - 2)
                if first and s == 0:
                    a_recip(NP * G - 1)
                if first and s == 2:
                    y_out(G)
                if (not (first and s == 0)) and not (drain and s >= 1):
                    wait(dve, b_e, n)
                    if first and s == 1:
                        wait(dve, a_p, NP * G)
                    wait(dve, b_p, n - 1)
                    V.reciprocal(rsum[:, :], sums[:, :]).then_inc(b_rs, 1)
                if not drain and s < 4:
                    b_v_rows(g, s, 1)
                if first and s < 2:
                    a_low(NP * G + s - 2)
                if lag2:
                    wait(dve, b_ohi, n - 1)
                    V.tensor_tensor(oT_lo[:, :], o_ps[:, :], oT_hi[:, :].bitcast(F32), ALU.subtract).then_inc(b_olo, 1)
                if s == 2 and not first:
                    wait(dve, b_pj, NP * g)
                    bias = bias_b[:, :].rearrange("p (a d) -> p a d", a=1).broadcast_to([P, 2, D])
                    for j in range(2):
                        V.tensor_tensor(near0[:, j, :].rearrange("p (a d) -> p a d", a=2),
                                        y_ps[j][:, :].rearrange("p (a d) -> p a d", a=2), bias, ALU.add).then_inc(b_z, 1)
                if not first:
                    for j in range(2):
                        if s == 4 + j or drain and s == 2:
                            wait(dve, b_z, 2 * g)
                            if j == 1:
                                wait(dve, b_x, 2 * g - 1)
                            add_rows(g - 1, j, near0[:, j, :], b_x)
                if not drain and s in (1, 3):
                    norm_stats(G + g + 1, (g + 1) % G, (0, 1) if s == 1 else (2, 3))
                if not drain and s in (5, 6):
                    norm_apply(G + g + 1, (g + 1) % G, (ln_T, 2 * (G + g) + 2), (0, 1) if s == 5 else (2, 3))
                if first and s == 7:
                    wait(dve, a_x, 2 * G)
                if s == NP - 1:
                    xnT_low(G + g + 1)

            for s in range(NP):
                b_slot(0, s, first=True)
            with dve.Fori(1, G) as g:
                for s in range(NP):
                    b_slot(g, s)
            dve.wait_ge(ld_top, 16)

            def c_weights(part):
                for n in part:
                    what, t, kt = C_PREP[n]
                    dve.wait_ge(cw_hi, n + 1)
                    bank = C_BANKS[n]
                    if what == "up":
                        i = V.tensor_tensor(wiT_lo[:, kt, t * P:t * P + 512], bank[:, :],
                                            wiT_hi[:, kt, t * P:t * P + 512].bitcast(F32), ALU.subtract)
                    elif what == "down":
                        lo, hi = (w[:, t:t + 2, :].rearrange("p a d -> p (a d)") for w in (wdT_lo, wdT_hi))
                        i = V.tensor_tensor(lo, bank[:, :], hi.bitcast(F32), ALU.subtract)
                    elif what in ("lb1", "lb2"):
                        third = (lb1T if what == "lb1" else lb2T)[64:96, t * P:t * P + 512]
                        i = V.tensor_tensor(third, bank[64:96, :], third.bitcast(F32), ALU.subtract)
                    else:
                        for j in range(4):
                            i = V.tensor_tensor(laT_lo[:, :, 32 * j:32 * j + 32],
                                                bank[:, 0:64].rearrange("p (k r) -> p k r", k=KD),
                                                laT_hi[:, :, 32 * j:32 * j + 32].bitcast(F32), ALU.subtract)
                    i.then_inc(cw_lo, 1)

            for s in range(2):
                b_slot(G, s, drain=True)
                c_weights(C_PARTS[s])

            def c_slot(g, s, first=False, drain=False):
                n = NF * g + s
                if not drain:
                    if s == 3:
                        wait(dve, ln_bn, 2 * G + g + 2)
                    if s > 0:
                        c_expert0(g, s, n)
                    if s == 3:
                        norm_moments()
                if s == NF - 1:
                    xnT_low(2 * G + g + 1)
                if not (first and s < 2) and not (drain and s >= 2):
                    p = (s - 2) % NF
                    wait(dve, c_ghi, n - 1)
                    V.tensor_tensor(tile_lo[p % 2][:, :], hid[:, :], tile_hi[p % 2][:, :].bitcast(F32),
                                    ALU.subtract).then_inc(c_glo, 1)
                if not (first and s < 1) and not (drain and s >= 1):
                    p = (s - 1) % NF
                    wait(dve, c_r1, n)
                    wait(dve, c_glo, n - 1)
                    V.scalar_tensor_tensor(hid[:, :], relu1[:, :], top_sb[:, 1:2], hid0[:, p % 2, :], ALU.mult,
                                           ALU.add).then_inc(c_g, 1)
                if not drain and s == 0:
                    wait(dve, c_thi, g + 1)
                    V.tensor_tensor(lowT[32:64, :], low_ps[32:64, :], lowT[32:64, :].bitcast(F32),
                                    ALU.subtract).then_inc(c_tlo, 1)
                    if first:
                        c_weights(C_PARTS[2])
                    c_expert0(g, s, n)
                    if first:
                        b_slot(G, 2, drain=True)
                if s == 2 and not first:
                    wait(dve, c_dn, NF * g)
                    for j in range(2):
                        add_rows(g - 1, j, y_ps[j][:, :], c_x)
                if not drain and s in (0, 1):
                    norm_stats(2 * G + g + 1, (g + 1) % G, (0, 1) if s == 0 else (2, 3))
                if not drain and s in (4, 5):
                    norm_apply(2 * G + g + 1, (g + 1) % G, (ln_T, 2 * (2 * G + g) + 2), (0, 1) if s == 4 else (2, 3))
                if first and s == NF - 1:
                    wait(dve, b_x, 2 * G)

            def c_expert0(g, s, n):
                wait(dve, c_u, n + 1)
                wait(dve, c_g, n - 1)
                V.tensor_scalar(hid0[:, s % 2, :], up_ps[s % 4][:, :], 0.0, top_sb[:, 0:1], ALU.max,
                                ALU.mult).then_inc(c_g0, 1)

            for s in range(NF):
                c_slot(0, s, first=True)
            with dve.Fori(1, G) as g:
                for s in range(NF):
                    c_slot(g, s)
            for s in range(3):
                c_slot(G, s, drain=True)


INPUTS = ["x", "ctx_512", "L0_attn_w_qkv", "L0_attn_w_proj", "L0_attn_b_proj", "L0_xattn_Wq", "L0_xattn_Wk",
          "L0_xattn_Wv", "L0_xattn_Wo", "L0_xattn_bo", "L0_ffn_wi_w", "L0_ffn_wo_w", "L0_ffn_lora_As",
          "L0_ffn_lora_Bs", "L0_ffn_top_k_indices", "L0_ffn_top_k_values"]


def kernel(**inputs):
    import concourse.bacc as bacc
    from concourse.bass_utils import run_bass_kernel_spmd

    nc = bacc.Bacc("TRN2", target_bir_lowering=False, num_devices=1)
    arrays, args = {}, []
    for name in INPUTS:
        a = np.ascontiguousarray(inputs[name])
        arrays[f"in_{name}"] = a
        args.append(nc.dram_tensor(f"in_{name}", a.shape, mybir.dt.from_np(a.dtype), kind="ExternalInput").ap())
    out = nc.dram_tensor("out", (B, NT, D), F32, kind="ExternalOutput").ap()
    build(nc, *args, out)
    r = run_bass_kernel_spmd(nc, [arrays], core_ids=[0])
    return r.results[0]["out"]
```

```python
import numpy as np
import concourse.bass as bass
from concourse import mybir
from concourse.alu_op_type import AluOpType as ALU

F32 = mybir.dt.float32
F32R = mybir.dt.float32r
BF16 = mybir.dt.bfloat16
I16 = mybir.dt.int16
I32 = mybir.dt.int32
ACT = mybir.ActivationFunctionType
AX = mybir.AxisListType.X

P = 128
B, NT, D = 16, 128, 256
H, DH = 16, 64
E = H * DH
F = 1024
CTX = 128
RANK = 16
GB = 4
G = B // GB
TOK = GB * NT
KD = D // P
NP = H // 2
NF = F // P
FIX = 4096.0
GROW = 1.0 + 2.0 ** -22
LOW = -(8.0 * FIX - 1.0)
EPS = 1e-5


def sbuf_map(nc):
    state = {"at": (nc.sbuf_base + 63) // 64 * 64}

    def place(name, shape, dtype, at=None):
        nbytes = int(np.prod(shape[1:])) * mybir.dt.size(dtype)
        nbytes = (nbytes + 31) // 32 * 32
        if at is None:
            at = state["at"]
            state["at"] = at + nbytes
        return nc.alloc_sbuf_tensor_at(name, list(shape), dtype, offset=at), at, at + nbytes

    return place, state


def block_index(s):
    return 4 * s if s < 4 else 16 + 2 * (s - 4)


BLOCKS = block_index(8)


def build(nc, x, ctx, w_qkv, w_proj, b_proj, Wq, Wk, Wv, Wo, bo, wi_w, wo_w, lora_As, lora_Bs,
          top_i, top_v, out):
    place, mem = sbuf_map(nc)

    def sb(name, shape, dtype, at=None):
        return place(name, shape, dtype, at)[0]

    x_sb = sb("x_sb", [P, B, D], F32)
    region_a = mem["at"]
    wqkvT_hi = sb("wqkvT_hi", [P, KD, 3 * E], F32R)
    wqkvT_lo = sb("wqkvT_lo", [P, KD, 3 * E], F32R)
    wpT_hi = sb("wpT_hi", [P, NP, D], F32R)
    wpT_lo = sb("wpT_lo", [P, NP, D], F32R)
    region_b = mem["at"]
    wq_hi = sb("wq_hi", [P, KD, E], F32R)
    wq_lo = sb("wq_lo", [P, KD, E], F32R)
    wk_hi = sb("wk_hi", [P, E], F32R)
    wk_lo = sb("wk_lo", [P, E], F32R)
    wv_hi = sb("wv_hi", [P, E], F32R)
    wv_lo = sb("wv_lo", [P, E], F32R)
    wo_hi = sb("wo_hi", [P, NP, D], F32R)
    wo_lo = sb("wo_lo", [P, NP, D], F32R)
    wqkv_raw, _, nxt = place("wqkv_raw", [P, 3 * NP, D], F32, at=region_b)
    wp_raw, _, nxt = place("wp_raw", [P, KD, E], F32, at=nxt)
    raw_b = sb("raw_b", [P, E], F32)
    xn = sb("xn", [P, GB, D], F32)
    xnT_hi = sb("xnT_hi", [P, KD, TOK], F32R)
    xnT_lo = sb("xnT_lo", [P, KD, TOK], F32R)
    v_sb = sb("v_sb", [P, GB, E], F32)
    q_sb = sb("q_sb", [P, 2, TOK], F32)
    k_sb = sb("k_sb", [P, 2, TOK], F32)
    e_sb = sb("e_sb", [P, 8, NT], F32)
    p_int = sb("p_int", [P, 8, NT], I16)
    s_sgn = sb("s_sgn", [P, 2, TOK], BF16)
    o_sgn = sb("o_sgn", [P, TOK], BF16)
    aT_sb = sb("aT_sb", [P, 8, NT], F32)
    oT_hi = sb("oT_hi", [P, TOK], F32R)
    oT_lo = sb("oT_lo", [P, TOK], F32R)
    sgn = sb("sgn", [P, 2, TOK], BF16)
    ri = sb("ri", [P, 2, TOK], I16)
    near0 = sb("near0", [P, 2, TOK], F32)
    si = sb("si", [P, 2, TOK], I16)
    oi = sb("oi", [P, TOK], I16)
    zi = sb("zi", [P, TOK], I16)
    ident = sb("ident", [P, P], F32)
    ident_b = sb("ident_b", [P, P], BF16)
    bias_a = sb("bias_a", [P, D], F32)
    bn_st = sb("bn_st", [P, GB, 6], F32)
    mv = sb("mv", [P, GB, 2], F32)
    veps = sb("veps", [P, GB], F32)
    rstd = sb("rstd", [P, GB], F32)
    mhalf = sb("mhalf", [P, GB], F32)
    sums = sb("sums", [P, 8], F32)
    rsum = sb("rsum", [P, 8], F32)
    rsc = sb("rsc", [P, 8], F32)
    mx = sb("mx", [P, 8], F32)
    neg_max = sb("neg_max", [P, 8], F32)
    bias_b = sb("bias_b", [P, D], F32)
    growth = sb("growth", [P, 8], F32)
    top_sb = sb("top_sb", [P, 2], F32)

    ctx_sb, _, nxt = place("ctx_sb", [P, GB, CTX], F32, at=region_a)
    cT_hi, _, nxt = place("cT_hi", [P, TOK], F32R, at=nxt)
    cT_lo, _, nxt = place("cT_lo", [P, TOK], F32R, at=nxt)
    p_f, _, nxt = place("p_f", [P, 8, NT], F32, at=nxt)
    wi_raw, _, nxt = place("wi_raw", [P, NF, D], F32, at=nxt)
    wd_raw, _, nxt = place("wd_raw", [P, KD, F], F32, at=nxt)
    lb_raw, _, nxt = place("lb_raw", [P, NF, 2, RANK], F32, at=nxt)
    lb1, _, nxt = place("lb1", [P, NF, 3, 2, RANK], F32, at=nxt)
    lb2, _, nxt = place("lb2", [P, NF, 3, 2, RANK], F32, at=nxt)
    la_raw, _, nxt = place("la_raw", [2 * RANK, D], F32, at=nxt)
    idx_sb, _, nxt = place("idx_sb", [1, 2], I32, at=nxt)
    hid0, _, nxt = place("hid0", [P, 2, TOK], F32, at=nxt)
    relu1, _, nxt = place("relu1", [P, TOK], F32, at=nxt)
    hid, _, nxt = place("hid", [P, TOK], F32, at=nxt)
    lowT, _, nxt = place("lowT", [96, TOK], F32R, at=nxt)
    assert nxt <= region_a + 4 * KD * 3 * E * 2
    lb1T, _, nxt = place("lb1T", [96, F], F32R, at=nxt)
    lb2T, _, nxt = place("lb2T", [96, F], F32R, at=nxt)
    laT_hi, _, nxt = place("laT_hi", [P, KD, P], F32R, at=nxt)
    laT_lo, _, nxt = place("laT_lo", [P, KD, P], F32R, at=nxt)
    oT2_hi, _, nxt = place("oT2_hi", [P, TOK], F32R, at=nxt)
    oT2_lo, _, nxt = place("oT2_lo", [P, TOK], F32R, at=nxt)
    assert nxt <= region_b
    tile_hi, tile_lo = (oT_hi, oT2_hi), (oT_lo, oT2_lo)
    wiT_hi, _, nxt = place("wiT_hi", [P, KD, F], F32R, at=region_b)
    wiT_lo, _, nxt = place("wiT_lo", [P, KD, F], F32R, at=nxt)
    wdT_hi, _, nxt = place("wdT_hi", [P, NF, D], F32R, at=nxt)
    wdT_lo, _, nxt = place("wdT_lo", [P, NF, D], F32R, at=nxt)
    assert nxt <= region_b + 4 * 8 * E
    assert mem["at"] <= nc.sbuf_usable_end, mem["at"] - nc.sbuf_usable_end

    banks = [nc.alloc_psum_tensor(f"bank{i}", [P, 512], F32) for i in range(8)]
    y_ps = banks[0:2]
    proj_ps = banks[2:4]
    s_ps = banks[4:6]
    t_ps = banks[6]
    o_ps = banks[7]
    one_ps = banks[2]
    pT_ps = (banks[3], banks[6])
    low_ps = banks[2]
    up_ps = banks[4:8]

    def sem(name):
        return nc.alloc_semaphore(name)

    ld_x0, ld_xr, ld_wq, ld_wk, ld_wv, ld_wp, ld_b = (
        sem(n) for n in ("ld_x0", "ld_xr", "ld_wq", "ld_wk", "ld_wv", "ld_wp", "ld_b"))
    ld_wq2, out_done = sem("ld_wq2"), sem("out_done")
    ld_raw, ld_bhi, ld_bb = sem("ld_raw"), sem("ld_bhi"), sem("ld_bb")
    ld_ctx, ld_cw, ld_idx, ld_top = sem("ld_ctx"), sem("ld_cw"), sem("ld_idx"), sem("ld_top")
    wb_lo, g_tick = sem("wb_lo"), sem("g_tick")
    b_cT, b_chi, b_clo, b_blk, b_q, b_k, b_v = (
        sem(n) for n in ("b_cT", "b_chi", "b_clo", "b_blk", "b_q", "b_k", "b_v"))
    b_S, b_mx, b_nm, b_e, b_rs, b_p, b_T = (sem(n) for n in ("b_S", "b_mx", "b_nm", "b_e", "b_rs", "b_p", "b_T"))
    b_pT, b_av, b_ohi, b_olo, b_pj = (sem(n) for n in ("b_pT", "b_av", "b_ohi", "b_olo", "b_pj"))
    b_z, b_x = sem("b_z"), sem("b_x")
    g_lb, cw_T, cw_hi, cw_lo = sem("g_lb"), sem("cw_T"), sem("cw_hi"), sem("cw_lo")
    c_t, c_thi, c_tlo, c_u, c_u2 = (sem(n) for n in ("c_t", "c_thi", "c_tlo", "c_u", "c_u2"))
    c_g0, c_r1, c_g, c_ghi, c_glo, c_dn, c_x = (sem(n) for n in ("c_g0", "c_r1", "c_g", "c_ghi", "c_glo", "c_dn", "c_x"))
    g_const, g_rstd = sem("g_const"), sem("g_rstd")
    w_T, w_hi, w_lo = sem("w_T"), sem("w_hi"), sem("w_lo")
    idb = sem("idb")
    ln_bn, ln_mv, ln_xn, ln_T, ln_hi, ln_lo = (sem(n) for n in ("ln_bn", "ln_mv", "ln_xn", "ln_T", "ln_hi", "ln_lo"))
    g_veps = sem("g_veps")
    a_blk, a_sgn, a_ri, a_fx = sem("a_blk"), sem("a_sgn"), sem("a_ri"), sem("a_fx")
    a_S, a_ssgn, a_si, a_clip, a_e = (sem(n) for n in ("a_S", "a_ssgn", "a_si", "a_clip", "a_e"))
    a_rs, a_rsc, a_p, a_T, a_aT = (sem(n) for n in ("a_rs", "a_rsc", "a_p", "a_T", "a_aT"))
    a_av, a_osgn, a_oi, a_ohi, a_olo, a_pj = (sem(n) for n in ("a_av", "a_osgn", "a_oi", "a_ohi", "a_olo", "a_pj"))
    a_z, a_zn, a_zi, a_zf, a_x = (sem(n) for n in ("a_z", "a_zn", "a_zi", "a_zf", "a_x"))

    def wait(eng, s, value):
        if isinstance(value, int) and value <= 0:
            return
        eng.wait_ge(s, value)

    PREP = []
    for sec in range(3):
        for half in range(2):
            for kt in range(KD):
                PREP.append(("qkv", sec * 8 + half * 4, kt))
    for et in range(0, NP, 2):
        PREP.append(("proj", et, None))
    PREP_BANKS = [banks[i] for i in (0, 1, 2, 3, 4, 5, 6, 7, 0, 1, 6, 7, 0, 1, 0, 1)]
    PREP_PARTS = [range(0, 8), range(8, 10), range(10, 14), range(14, len(PREP))]

    B_CHUNKS = [(Wq.rearrange("(t p) e -> p t e", p=P)[:, i, :], wq_hi[:, i, :], wq_lo[:, i, :]) for i in range(KD)]
    B_CHUNKS += [(Wk, wk_hi[:, :], wk_lo[:, :]), (Wv, wv_hi[:, :], wv_lo[:, :])]
    B_CHUNKS += [(Wo.rearrange("(t p) d -> p t d", p=P)[:, 4 * i:4 * i + 4, :], wo_hi[:, 4 * i:4 * i + 4, :],
                  wo_lo[:, 4 * i:4 * i + 4, :]) for i in range(2)]

    C_PREP = [("la", 0, None)] + [("up", t, kt) for t in (0, 4) for kt in range(KD)]
    C_PREP += [("lb1", t, None) for t in (0, 4)] + [("lb2", t, None) for t in (0, 4)]
    C_PREP += [("down", t, None) for t in range(0, NF, 2)]
    C_BANKS = [banks[i] for i in (2, 4, 5, 2, 4, 5, 4, 5, 4, 6, 7, 3, 6)]
    C_PARTS = [range(0, 6), range(6, 9), range(9, len(C_PREP))]

    with nc.Block() as block:

        @block.sync
        def _(sp):
            rows = w_qkv.rearrange("(t p) d -> p t d", p=P)
            sp.dma_start(wqkv_raw[:, 0:4, :], rows[:, 0:4, :]).then_inc(ld_wq, 16)
            sp.dma_start(x_sb[:, 0:GB, :], x[0:GB].rearrange("b p d -> p b d")).then_inc(ld_x0, 16)
            sp.dma_start(wqkv_raw[:, 4:8, :], rows[:, 4:8, :]).then_inc(ld_wq2, 16)
            for i, s_ in ((1, ld_wk), (2, ld_wv)):
                sp.dma_start(wqkv_raw[:, 8 * i:8 * i + 8, :], rows[:, 8 * i:8 * i + 8, :]).then_inc(s_, 16)
            sp.dma_start(wp_raw[:, :, :], w_proj.rearrange("(t p) e -> p t e", p=P)).then_inc(ld_wp, 16)
            for g in range(1, G):
                sp.dma_start(x_sb[:, g * GB:(g + 1) * GB, :],
                             x[g * GB:(g + 1) * GB].rearrange("b p d -> p b d")).then_inc(ld_xr, 16)
            sp.dma_start(bias_a[:, :], b_proj.partition_broadcast(P)).then_inc(ld_b, 16)
            sp.dma_start(bias_b[:, :], bo.partition_broadcast(P)).then_inc(ld_bb, 16)
            sp.dma_start(top_sb[:, :], top_v.partition_broadcast(P)).then_inc(ld_top, 16)
            sp.wait_ge(w_lo, len(PREP))
            for n, (src, hi, lo) in enumerate(B_CHUNKS):
                wait(sp, wb_lo, n)
                dst = raw_b[:, :] if len(src.shape) == 2 else raw_b[:, :].rearrange("p (a d) -> p a d", d=src.shape[2])
                sp.dma_start(dst, src).then_inc(ld_raw, 16)
            sp.wait_ge(a_blk, BLOCKS * G)
            sp.dma_start(idx_sb[:, :], top_i.rearrange("(a k) -> a k", a=1)).then_inc(ld_idx, 16)
            for g in range(G):
                wait(sp, b_cT, g)
                sp.dma_start(ctx_sb[:, :, :], ctx[g * GB:(g + 1) * GB].rearrange("b p d -> p b d")).then_inc(ld_ctx, 16)
                if g == 0:
                    sp.dma_start(wi_raw[:, :, :], wi_w.rearrange("(t p) d -> p t d", p=P)).then_inc(ld_cw, 16)
                    sp.dma_start(wd_raw[:, :, :], wo_w.rearrange("(t p) f -> p t f", p=P)).then_inc(ld_cw, 16)
                    sp.wait_ge(ld_idx, 16)
                    for k in range(2):
                        expert = sp.value_load(idx_sb[0:1, k:k + 1], min_val=0, max_val=lora_As.shape[0] - 1)
                        sp.dma_start(la_raw[k * RANK:(k + 1) * RANK, :],
                                     lora_As[bass.ds(expert, 1), :, :].rearrange("a r d -> (a r) d")).then_inc(ld_cw, 16)
                        sp.dma_start(lb_raw[:, :, k, :],
                                     lora_Bs[bass.ds(expert, 1), :, :].rearrange("a (t p) r -> p (a t) r", p=P)).then_inc(ld_cw, 16)
            for n in range(2 * G):
                sp.wait_ge(c_x, n + 1)
                sp.dma_start(out[2 * n:2 * n + 2].rearrange("b p d -> p b d"),
                             x_sb[:, 2 * n:2 * n + 2, :]).then_inc(out_done, 16)
            sp.wait_ge(out_done, 16 * 2 * G)

        @block.gpsimd
        def _(pool):
            nc.gpsimd.memset(ident[:, :], 0.0).then_inc(g_const, 1)
            nc.gpsimd.memset(mhalf[:, :], -0.5).then_inc(g_const, 1)
            nc.gpsimd.memset(growth[:, :], FIX * GROW).then_inc(g_const, 1)
            pool.wait_ge(g_const, 3)
            nc.gpsimd.affine_select(out=ident[:, :], in_=ident[:, :], compare_op=ALU.not_equal, fill=1.0,
                                    base=0, pattern=[[-1, P]], channel_multiplier=1).then_inc(g_const, 1)

            def inv_std(n):
                wait(pool, ln_mv, n + 1)
                nc.gpsimd.sem_inc(g_tick, 1)
                nc.gpsimd.tensor_scalar(veps[:, :], mv[:, :, 1], EPS, None, ALU.add).then_inc(g_veps, 1)
                wait(pool, g_veps, n + 1)
                nc.gpsimd.tensor_tensor(rstd[:, :], veps[:, :], mhalf[:, :], ALU.pow).then_inc(g_rstd, 1)

            def a_weights(n):
                wait(pool, a_rs, n + 1)
                nc.gpsimd.tensor_tensor(rsc[:, :], rsum[:, :], growth[:, :], ALU.mult).then_inc(a_rsc, 1)
                wait(pool, a_T, n)
                wait(pool, a_rsc, n + 1)
                nc.gpsimd.sem_inc(g_tick, 1)
                for t in range(8):
                    i = nc.gpsimd.tensor_scalar(p_int[:, t, :], e_sb[:, t, :], rsc[:, t:t + 1], -0.5,
                                                ALU.mult, ALU.add)
                i.then_inc(a_p, 1)

            def a_add_rows(g, j):
                wait(pool, a_zf, 2 * (g - 1) + j + 1)
                nc.gpsimd.sem_inc(g_tick, 1)
                xx = x_sb[:, bass.ds((g - 1) * GB + 2 * j, 2), :].rearrange("p a d -> p (a d)")
                nc.gpsimd.tensor_tensor(xx, xx, raw_b[:, j * TOK:(j + 1) * TOK], ALU.add).then_inc(a_x, 1)

            def a_slot(g, s, first=False):
                if not (first and s == 0):
                    a_weights(NP * g + s - 1)
                if not first and s in (5, 7):
                    a_add_rows(g, (s - 5) // 2)
                if s == 2:
                    inv_std(g + 1)

            inv_std(0)
            nc.gpsimd.sem_inc(a_x, 2)
            for s in range(NP):
                a_slot(0, s, first=True)
                if s == 2:
                    pool.wait_ge(w_lo, len(PREP))
                    for src, hi, lo in B_CHUNKS:
                        nc.gpsimd.dma_start(hi, src).then_inc(ld_bhi, 16)
                if s == 3:
                    pool.wait_ge(ld_bhi, 16 * len(B_CHUNKS))
                for n in ((), (), (), (0,), (1,), (2,), (3,), (4, 5))[s]:
                    _, hi, lo = B_CHUNKS[n]
                    raw = raw_b[:, :] if len(hi.shape) == 2 else raw_b[:, :].rearrange("p (a d) -> p a d", d=hi.shape[2])
                    pool.wait_ge(ld_raw, 16 * (n + 1))
                    nc.gpsimd.tensor_tensor(lo, raw, hi.bitcast(F32), ALU.subtract).then_inc(wb_lo, 1)
            with pool.Fori(1, G) as g:
                for s in range(NP):
                    a_slot(g, s)
            a_weights(NP * G - 1)

            def b_weights(n):
                wait(pool, b_rs, n + 1)
                wait(pool, b_T, n)
                nc.gpsimd.sem_inc(g_tick, 1)
                for t in range(8):
                    i = nc.gpsimd.tensor_scalar(p_f[:, t, :], e_sb[:, t, :], rsum[:, t:t + 1], 0.0, ALU.mult, ALU.add)
                i.then_inc(b_p, 1)

            def b_slot(g, s, first=False):
                if first and s in (5, 7):
                    a_add_rows(G, (s - 5) // 2)
                if not (first and s == 0):
                    b_weights(NP * g + s - 1)
                if s == 4:
                    inv_std(G + g + 1)

            for s in range(NP):
                b_slot(0, s, first=True)
                if s == 1:
                    pool.wait_ge(ld_cw, 16 * 6)
                    nc.gpsimd.memset(lb1[:, :, :, 1, :], 0.0).then_inc(g_lb, 1)
                    for j in range(3):
                        nc.gpsimd.tensor_copy(lb1[:, :, j, 0, :], lb_raw[:, :, 0, :]).then_inc(g_lb, 1)
                        nc.gpsimd.tensor_scalar(lb2[:, :, j, 0, :], lb_raw[:, :, 0, :], -1.0, 0.0, ALU.mult,
                                                ALU.add).then_inc(g_lb, 1)
                        nc.gpsimd.tensor_copy(lb2[:, :, j, 1, :], lb_raw[:, :, 1, :]).then_inc(g_lb, 1)
            with pool.Fori(1, G) as g:
                for s in range(NP):
                    b_slot(g, s)
            b_weights(NP * G - 1)
            pool.wait_ge(b_z, 2 * G)
            pool.wait_ge(b_x, 2 * G - 2)
            nc.gpsimd.sem_inc(g_tick, 1)
            for j in range(2):
                xx = x_sb[:, (G - 1) * GB + 2 * j:(G - 1) * GB + 2 * j + 2, :].rearrange("p a d -> p (a d)")
                nc.gpsimd.tensor_tensor(xx, xx, near0[:, j, :], ALU.add).then_inc(b_x, 1)
            for g in range(G):
                inv_std(2 * G + g + 1)

        @block.tensor
        def _(pe):
            def split3(out_, w_pair, m_pair, first, last, **kw):
                (wh, wl), (mh, ml) = w_pair, m_pair
                pe.matmul(out_, wl, mh, start=first, stop=False, **kw)
                pe.matmul(out_, wh, ml, start=False, stop=False, **kw)
                return pe.matmul(out_, wh, mh, start=False, stop=last, **kw)

            def a_weights_T(part):
                for n in part:
                    what, t, kt = PREP[n]
                    if what == "qkv":
                        if t % 8 == 0 and kt == 0:
                            pe.wait_ge((ld_wq, ld_wk, ld_wv)[t // 8], 16)
                        elif t == 4 and kt == 0:
                            pe.wait_ge(ld_wq2, 16)
                    elif t == 0:
                        pe.wait_ge(ld_wp, 16)
                    wait(pe, w_lo, n - 7 if n < 10 else n - 3 if n < 14 else n - 1)
                    for j in range(4):
                        if what == "qkv":
                            src = wqkv_raw[:, t + j, kt * P:(kt + 1) * P]
                        else:
                            src = wp_raw[:, j % 2, (t + j // 2) * P:(t + j // 2 + 1) * P]
                        last = pe.transpose(PREP_BANKS[n][:, j * P:(j + 1) * P], src, ident[:, :])
                    last.then_inc(w_T, 1)

            pe.wait_ge(g_const, 4)
            a_weights_T(PREP_PARTS[0])

            def normed_T(n, prev_reads):
                wait(pe, ln_xn, n + 1)
                prev_reads()
                for kt in range(KD):
                    for b in range(GB):
                        last = pe.transpose(proj_ps[kt][:, b * P:(b + 1) * P], xn[:, b, kt * P:(kt + 1) * P],
                                            ident[:, :])
                    last.then_inc(ln_T, 1)

            def a_block(g, m, w0, moving_tokens):
                if m < 2:
                    wait(pe, ln_lo, 2 * g + 2)
                else:
                    wait(pe, a_ri, BLOCKS * g + m - 1)
                ps = proj_ps[m % 2]
                for kt in range(KD):
                    if moving_tokens:
                        wp = [w[:, kt, w0:w0 + P] for w in (wqkvT_hi, wqkvT_lo)]
                        mp = [t[:, kt, :] for t in (xnT_hi, xnT_lo)]
                    else:
                        b, col = w0
                        wp = [t[:, kt, b * P:(b + 1) * P] for t in (xnT_hi, xnT_lo)]
                        mp = [w[:, kt, col:col + 512] for w in (wqkvT_hi, wqkvT_lo)]
                    last = split3(ps[:, :], wp, mp, kt == 0, kt == KD - 1)
                last.then_inc(a_blk, 1)

            def a_transpose(n):
                wait(pe, a_p, n + 1)
                wait(pe, a_aT, n)
                for t in range(8):
                    last = pe.transpose(t_ps[:, t * 64:(t + 1) * 64].bitcast(BF16),
                                        p_int[:, t, :].bitcast(BF16), ident_b[:, :])
                last.then_inc(a_T, 1)

            def a_attend(n, p, v_count):
                wait(pe, a_aT, n + 1)
                wait(pe, a_fx, v_count)
                wait(pe, a_oi, n)
                for b in range(GB):
                    for hh in range(2):
                        h0 = (2 * p + hh) * DH
                        last = pe.matmul(o_ps[hh * DH:(hh + 1) * DH, b * P:(b + 1) * P], v_sb[:, b, h0:h0 + DH],
                                         aT_sb[:, GB * hh + b, :], start=True, stop=True)
                last.then_inc(a_av, 1)

            def project_out(n, p, ready, done, weights, y_free, batches=range(GB)):
                wait(pe, ready, n + 1)
                if p == 0:
                    wait(pe, *y_free)
                for b in batches:
                    first = p == 0 and b % 2 == 0
                    last = split3(y_ps[b // 2][:, (b % 2) * D:(b % 2 + 1) * D],
                                  [t[:, b * P:(b + 1) * P] for t in (oT_hi, oT_lo)],
                                  [w[:, p, :] for w in weights], first, p == NP - 1, skip_group_check=True)
                if GB - 1 in batches:
                    last.then_inc(done, 1)

            def a_scores(n, s, blk):
                wait(pe, a_fx, blk)
                wait(pe, a_si, 2 * n)
                for b in range(GB):
                    for hh in range(2):
                        last = pe.matmul(s_ps[hh][:, b * P:(b + 1) * P],
                                         q_sb[hh * DH:(hh + 1) * DH, s % 2, b * P:(b + 1) * P],
                                         k_sb[hh * DH:(hh + 1) * DH, s % 2, b * P:(b + 1) * P],
                                         start=True, stop=True)
                        if b == GB - 1:
                            last.then_inc(a_S, 1)

            def a_slot(g, s, first=False):
                n = NP * g + s
                base = block_index(s)
                a_block(g, base, s * P, True)
                a_block(g, base + 1, E + s * P, True)
                if first and s in (1, 2):
                    a_weights_T(PREP_PARTS[s + 1])
                if first:
                    wait(pe, w_lo, (10, 0, 12, len(PREP), 0, 0, 0, 0)[s])
                lag2 = not (first and s < 2)
                if lag2:
                    a_transpose(n - 2)
                if not (first and s < 3):
                    project_out(n - 3, (s - 3) % NP, a_olo, a_pj, (wpT_hi, wpT_lo), (a_z, 2 * g))
                if s == NP - 1:
                    normed_T(g + 1, lambda: wait(pe, a_ri, BLOCKS * (g + 1)))
                if lag2:
                    p = (s - 2) % NP
                    gg = g if s >= 2 else g - 1
                    a_attend(n - 2, p, BLOCKS * gg + (block_index(1) + 4 if p < 4 else block_index(3) + 4))
                if s < 4:
                    for i in range(2):
                        j = 2 * s + i
                        a_block(g, base + 2 + i, (j % 4, 2 * E + 512 * (j // 4)), False)
                a_scores(n, s, BLOCKS * g + base + 2)

            normed_T(0, lambda: wait(pe, w_lo, 4))
            a_weights_T(PREP_PARTS[1])
            pe.wait_ge(w_lo, 8)
            pe.wait_ge(idb, 1)
            for s in range(NP):
                a_slot(0, s, first=True)
            with pe.Fori(1, G) as g:
                for s in range(NP):
                    a_slot(g, s)

            pe.wait_ge(wb_lo, len(B_CHUNKS))

            def b_block(g, s, what, i=0):
                if what == "q":
                    wait(pe, ln_lo, 2 * (G + g) + 2)
                    if s == 0:
                        wait(pe, b_clo, g + 1)
                    elif s <= 4:
                        wait(pe, b_v, 8 * g + 2 * s)
                    else:
                        wait(pe, b_k, NP * g + s)
                    for kt in range(KD):
                        last = split3(one_ps[:, :], [w[:, kt, s * P:(s + 1) * P] for w in (wq_hi, wq_lo)],
                                      [t[:, kt, :] for t in (xnT_hi, xnT_lo)], kt == 0, kt == KD - 1)
                elif what == "k":
                    if s < 4:
                        wait(pe, b_v, 8 * g + 2 * s + 1)
                    else:
                        wait(pe, b_q, NP * g + s + 1)
                    last = split3(one_ps[:, :], [w[:, s * P:(s + 1) * P] for w in (wk_hi, wk_lo)],
                                  [t[:, :] for t in (cT_hi, cT_lo)], True, True)
                else:
                    if i == 0:
                        wait(pe, b_q, NP * g + s + 1)
                    else:
                        wait(pe, b_k, NP * g + s + 1)
                    b, col = (2 * s + i) % 4, 512 * ((2 * s + i) // 4)
                    last = split3(one_ps[:, :], [t[:, b * P:(b + 1) * P] for t in (cT_hi, cT_lo)],
                                  [w[:, col:col + 512] for w in (wv_hi, wv_lo)], True, True)
                last.then_inc(b_blk, 1)

            def b_transpose(n):
                wait(pe, b_p, n + 1)
                if isinstance(n, int) and n == 0:
                    wait(pe, a_aT, NP * G)
                wait(pe, b_pT, n)
                for hh in range(2):
                    for b in range(GB):
                        last = pe.transpose(pT_ps[hh][:, b * P:(b + 1) * P], p_f[:, GB * hh + b, :], ident[:, :])
                last.then_inc(b_T, 1)

            def b_attend(n, p, v_count):
                wait(pe, b_pT, n + 1)
                wait(pe, b_v, v_count)
                if isinstance(n, int) and n == 0:
                    wait(pe, a_oi, NP * G)
                wait(pe, b_olo, n)
                for b in range(GB):
                    for hh in range(2):
                        h0 = (2 * p + hh) * DH
                        last = pe.matmul(o_ps[hh * DH:(hh + 1) * DH, b * P:(b + 1) * P], v_sb[:, b, h0:h0 + DH],
                                         aT_sb[:, GB * hh + b, :], start=True, stop=True)
                last.then_inc(b_av, 1)

            def b_scores(g, n, s):
                wait(pe, b_q, n + 1)
                wait(pe, b_k, n + 1)
                if isinstance(n, int) and n == 0:
                    wait(pe, a_si, 2 * NP * G)
                wait(pe, b_e, n)
                for b in range(GB):
                    for hh in range(2):
                        last = pe.matmul(s_ps[hh][:, b * P:(b + 1) * P],
                                         q_sb[hh * DH:(hh + 1) * DH, s % 2, b * P:(b + 1) * P],
                                         k_sb[hh * DH:(hh + 1) * DH, s % 2, b * P:(b + 1) * P],
                                         start=True, stop=True)
                        if b == GB - 1:
                            last.then_inc(b_S, 1)

            def b_slot(g, s, first=False, drain=False):
                n = NP * g + s
                lag2 = not (first and s < 2) and not (drain and s >= 2)
                if s == 0 and not drain:
                    wait(pe, ld_ctx, 16 * (g + 1))
                    wait(pe, ln_lo, 2 * (G + g) + 1)
                    for b in range(GB):
                        last = pe.transpose(one_ps[:, b * P:(b + 1) * P], ctx_sb[:, b, :], ident[:, :])
                    last.then_inc(b_cT, 1)
                def transposes():
                    if first and s < 2:
                        a_transpose(NP * G + s - 2)
                    if lag2:
                        if s == 0:
                            wait(pe, ln_lo, 2 * (G + g) + 2)
                        b_transpose(n - 2)

                def project(batches=range(GB)):
                    if first and s < 3:
                        project_out(NP * G + s - 3, NP + s - 3, a_olo, a_pj, (wpT_hi, wpT_lo), None, batches)
                    else:
                        project_out(n - 3, (s - 3) % NP, b_olo, b_pj, (wo_hi, wo_lo),
                                    (a_z, 2 * G) if first else (b_z, 2 * g), batches)

                def attend():
                    if first and s < 2:
                        a_attend(NP * G + s - 2, NP + s - 2, BLOCKS * (G - 1) + block_index(3) + 4)
                    if lag2:
                        p = (s - 2) % NP
                        gg = g if s >= 2 else g - 1
                        b_attend(n - 2, p, 8 * gg + (4 if p < 4 else 8))

                if drain:
                    transposes()
                    project()
                    attend()
                elif first and s == 0:
                    project((0, 1))
                    transposes()
                    b_block(g, s, "q")
                    project((2, 3))
                    b_block(g, s, "v", 0)
                    attend()
                    b_block(g, s, "k")
                elif s == 0:
                    transposes()
                    b_block(g, s, "q")
                    project((0, 1))
                    b_block(g, s, "v", 0)
                    project((2, 3))
                    b_block(g, s, "k")
                    attend()
                else:
                    b_block(g, s, "q")
                    transposes()
                    if s < 4:
                        b_block(g, s, "v", 0)
                    project()
                    b_block(g, s, "k")
                    attend()
                if not drain:
                    if s < 4:
                        b_block(g, s, "v", 1)
                    if s == NP - 1:
                        def free():
                            wait(pe, b_k, n + 1)
                            wait(pe, b_pT, n - 1)
                        normed_T(G + g + 1, free)
                    b_scores(g, n, s)

            for s in range(NP):
                b_slot(0, s, first=True)
            with pe.Fori(1, G) as g:
                for s in range(NP):
                    b_slot(g, s)
            def c_weights(part):
                for n in part:
                    what, t, kt = C_PREP[n]
                    wait(pe, cw_lo, n - 2 if n < 6 else n - 1 if n < 9 else 10 if n == 12 else 0)
                    for j in range(4):
                        if what == "up":
                            last = pe.transpose(C_BANKS[n][:, j * P:(j + 1) * P], wi_raw[:, t + j, kt * P:(kt + 1) * P],
                                                ident[:, :])
                        elif what == "down":
                            f0 = (t + j // 2) * P
                            last = pe.transpose(C_BANKS[n][:, j * P:(j + 1) * P], wd_raw[:, j % 2, f0:f0 + P], ident[:, :])
                        elif what in ("lb1", "lb2"):
                            src = (lb1 if what == "lb1" else lb2)[:, t + j, :, :, :].rearrange("p c k r -> p (c k r)")
                            last = pe.transpose(C_BANKS[n][0:96, j * P:(j + 1) * P], src, ident[:, :])
                        elif j < KD:
                            last = pe.transpose(C_BANKS[n][:, j * 32:(j + 1) * 32], la_raw[:, j * P:(j + 1) * P],
                                                ident[0:32, 0:32])
                    last.then_inc(cw_T, 1)

            for s in range(2):
                b_slot(G, s, drain=True)
                if s == 0:
                    pe.wait_ge(g_lb, 10)
                    pe.wait_ge(b_e, NP * G)
                c_weights(C_PARTS[s])

            def c_slot(g, s, first=False, drain=False):
                n = NF * g + s

                def up():
                    wait(pe, c_r1, n - 3)
                    u = up_ps[s % 4]
                    for kt in range(KD):
                        split3(u[:, :], [w[:, kt, s * P:(s + 1) * P] for w in (wiT_hi, wiT_lo)],
                               [t[:, kt, :] for t in (xnT_hi, xnT_lo)], kt == 0, False)
                    wait(pe, c_tlo, g + 1)
                    pe.matmul(u[:, :], lb1T[:, s * P:(s + 1) * P], lowT[:, :], start=False, stop=True).then_inc(c_u, 1)

                if first and s == 2:
                    wait(pe, cw_lo, len(C_PREP))
                if not drain and s > 0:
                    up()
                if s == NF - 1:
                    normed_T(2 * G + g + 1, lambda: wait(pe, c_tlo, g + 1))
                if not (first and s < 1) and not (drain and s >= 1):
                    p = (s - 1) % NF
                    wait(pe, c_g0, n)
                    pe.matmul(up_ps[p % 4][:, :], lb2T[:, p * P:(p + 1) * P], lowT[:, :], start=False, stop=True,
                              skip_group_check=True).then_inc(c_u2, 1)
                if not (first and s < 3):
                    p = (s - 3) % NF
                    wait(pe, c_glo, n - 2)
                    if p == 0 and first:
                        wait(pe, b_z, 2 * G)
                    elif p == 0:
                        wait(pe, c_x, 2 * g)
                    for b in range(GB):
                        last = split3(y_ps[b // 2][:, (b % 2) * D:(b % 2 + 1) * D],
                                      [t[p % 2][:, b * P:(b + 1) * P] for t in (tile_hi, tile_lo)],
                                      [w[:, p, :] for w in (wdT_hi, wdT_lo)], p == 0 and b % 2 == 0, p == NF - 1,
                                      skip_group_check=True)
                    last.then_inc(c_dn, 1)
                if s == 0 and not drain:
                    wait(pe, ln_lo, 2 * (2 * G + g) + 2)
                    if first:
                        pe.wait_ge(cw_lo, 4)
                    for kt in range(KD):
                        last = split3(low_ps[:, :], [w[:, kt, :] for w in (laT_hi, laT_lo)],
                                      [t[:, kt, :] for t in (xnT_hi, xnT_lo)], kt == 0, kt == KD - 1)
                    last.then_inc(c_t, 1)
                    if first:
                        b_slot(G, 2, drain=True)
                        pe.wait_ge(b_pT, NP * G)
                        pe.wait_ge(b_olo, NP * G)
                        c_weights(C_PARTS[2])
                        pe.wait_ge(cw_lo, 9)
                    up()

            for s in range(NF):
                c_slot(0, s, first=True)
            with pe.Fori(1, G) as g:
                for s in range(NF):
                    c_slot(g, s)
            for s in range(3):
                c_slot(G, s, drain=True)

        @block.scalar
        def _(act):
            def a_weights_high(part):
                for n in part:
                    what, t, kt = PREP[n]
                    act.wait_ge(w_T, n + 1)
                    if what == "qkv":
                        dst = wqkvT_hi[:, kt, t * P:t * P + 512]
                    else:
                        dst = wpT_hi[:, t:t + 2, :].rearrange("p a d -> p (a d)")
                    nc.scalar.activation(dst, PREP_BANKS[n][:, :], ACT.Copy,
                                         scale=FIX * GROW if what == "qkv" else 1.0).then_inc(w_hi, 1)

            a_weights_high(PREP_PARTS[0])

            def xnT_high(n):
                for kt in range(KD):
                    wait(act, ln_T, 2 * n + kt + 1)
                    nc.scalar.copy(xnT_hi[:, kt, :], proj_ps[kt][:, :]).then_inc(ln_hi, 1)

            def sign_of(g, m):
                wait(act, a_blk, BLOCKS * g + m + 1)
                wait(act, a_ri, BLOCKS * g + m - 1)
                nc.scalar.activation(sgn[:, m % 2, :], proj_ps[m % 2][:, :], ACT.Sign).then_inc(a_sgn, 1)

            def a_weightsT(n):
                wait(act, a_T, n + 1)
                wait(act, a_av, n)
                nc.scalar.activation(aT_sb[:, :, :].rearrange("p a t -> p (a t)"), t_ps[:, :].bitcast(I16),
                                     ACT.Copy, scale=GROW / FIX).then_inc(a_aT, 1)

            def a_exp(n, i):
                if i == 0:
                    wait(act, a_p, n)
                    wait(act, a_rs, n)
                wait(act, a_clip, 2 * n + 1 + i)
                for j in range(4):
                    t = 4 * i + j
                    last = nc.scalar.activation(e_sb[:, t, :], si[:, i, j * P:(j + 1) * P], ACT.Exp,
                                                scale=1.0 / FIX, accum_out=sums[:, t:t + 1])
                last.then_inc(a_e, 1)

            def a_out_sign(n):
                wait(act, a_av, n + 1)
                wait(act, a_oi, n)
                nc.scalar.activation(o_sgn[:, :], o_ps[:, :], ACT.Sign).then_inc(a_osgn, 1)

            def a_slot(g, s, first=False):
                n = NP * g + s
                base = block_index(s)
                sign_of(g, base)
                sign_of(g, base + 1)
                if first and s in (1, 2):
                    a_weights_high(PREP_PARTS[s + 1])
                lag2 = not (first and s < 2)
                if lag2:
                    a_weightsT(n - 2)
                if not (first and s == 0):
                    a_exp(n - 1, 0)
                    if s == NP - 1:
                        xnT_high(g + 1)
                    a_exp(n - 1, 1)
                if lag2:
                    a_out_sign(n - 2)
                if s < 4:
                    sign_of(g, base + 2)
                    sign_of(g, base + 3)
                for i in range(2):
                    wait(act, a_S, 2 * n + i + 1)
                    wait(act, a_si, 2 * n + i - 1)
                    nc.scalar.activation(s_sgn[:, i, :], s_ps[i][:, :], ACT.Sign).then_inc(a_ssgn, 1)

            xnT_high(0)
            a_weights_high(PREP_PARTS[1])
            for s in range(NP):
                a_slot(0, s, first=True)
            with act.Fori(1, G) as g:
                for s in range(NP):
                    a_slot(g, s)

            def b_slot(g, s, first=False, drain=False):
                n = NP * g + s
                lag2 = not (first and s < 2) and not (drain and s >= 2)
                if not drain:
                    if s == 0:
                        wait(act, b_cT, g + 1)
                        nc.scalar.copy(cT_hi[:, :], one_ps[:, :]).then_inc(b_chi, 1)
                    if first and s == 0:
                        a_weightsT(NP * G - 2)
                    wait(act, b_S, 2 * n - 2)
                    wait(act, b_blk, BLOCKS * g + block_index(s) + 1)
                    if first and s < 2:
                        wait(act, a_S, 2 * (NP * G + s) - 2)
                    nc.scalar.copy(q_sb[:, s % 2, :], one_ps[:, :]).then_inc(b_q, 1)
                if first and s == 1:
                    a_weightsT(NP * G - 1)
                if first and s == 0:
                    a_exp(NP * G - 1, 0)
                    a_exp(NP * G - 1, 1)
                if (not (first and s == 0)) and not (drain and s >= 1):
                    if first and s == 1:
                        wait(act, a_p, NP * G)
                    wait(act, b_p, n - 1)
                    wait(act, b_rs, n - 1)
                    for hh in range(2):
                        wait(act, b_nm, 2 * n - 1 + hh)
                        for t in range(GB * hh, GB * hh + GB):
                            last = nc.scalar.activation(e_sb[:, t, :], s_ps[hh][:, (t % 4) * P:(t % 4 + 1) * P], ACT.Exp,
                                                        bias=neg_max[:, t:t + 1], scale=DH ** -0.5,
                                                        accum_out=sums[:, t:t + 1])
                    last.then_inc(b_e, 1)
                if first and s < 2:
                    a_out_sign(NP * G + s - 2)
                if lag2:
                    wait(act, b_av, n - 1)
                    if first and s == 2:
                        wait(act, a_pj, NP * G)
                    wait(act, b_pj, n - 2)
                    nc.scalar.copy(oT_hi[:, :], o_ps[:, :]).then_inc(b_ohi, 1)
                if s == NP - 1:
                    xnT_high(G + g + 1)

            for s in range(NP):
                b_slot(0, s, first=True)
            with act.Fori(1, G) as g:
                for s in range(NP):
                    b_slot(g, s)
            def c_weights(part):
                for n in part:
                    what, t, kt = C_PREP[n]
                    act.wait_ge(cw_T, n + 1)
                    bank = C_BANKS[n]
                    if what == "up":
                        last = nc.scalar.copy(wiT_hi[:, kt, t * P:t * P + 512], bank[:, :])
                    elif what == "down":
                        last = nc.scalar.copy(wdT_hi[:, t:t + 2, :].rearrange("p a d -> p (a d)"), bank[:, :])
                    elif what in ("lb1", "lb2"):
                        last = nc.scalar.copy((lb1T if what == "lb1" else lb2T)[:, t * P:t * P + 512], bank[0:96, :])
                    else:
                        for j in range(4):
                            last = nc.scalar.copy(laT_hi[:, :, 32 * j:32 * j + 32],
                                                  bank[:, 0:64].rearrange("p (k r) -> p k r", k=KD))
                    last.then_inc(cw_hi, 1)

            for s in range(2):
                b_slot(G, s, drain=True)
                c_weights(C_PARTS[s])

            def c_slot(g, s, first=False, drain=False):
                n = NF * g + s
                if s == NF - 1:
                    xnT_high(2 * G + g + 1)
                if not (first and s < 1) and not (drain and s >= 1):
                    p = (s - 1) % NF
                    wait(act, c_u2, n)
                    wait(act, c_g, n - 1)
                    nc.scalar.activation(relu1[:, :], up_ps[p % 4][:, :], ACT.Relu).then_inc(c_r1, 1)
                if s == 0 and not drain:
                    wait(act, c_t, g + 1)
                    nc.scalar.copy(lowT[:, :], low_ps[0:96, :]).then_inc(c_thi, 1)
                    if first:
                        c_weights(C_PARTS[2])
                if not (first and s < 1) and not (drain and s >= 1):
                    wait(act, c_g, n)
                    if first and s == 1:
                        wait(act, b_pj, NP * G)
                    wait(act, c_dn, n - 2)
                    nc.scalar.copy(tile_hi[p % 2][:, :], hid[:, :]).then_inc(c_ghi, 1)

            for s in range(NF):
                c_slot(0, s, first=True)
            with act.Fori(1, G) as g:
                for s in range(NF):
                    c_slot(g, s)
            c_slot(G, 0, drain=True)

        @block.vector
        def _(dve):
            V = nc.vector

            def norm_stats(n, g, batches=range(GB)):
                for b in batches:
                    i = V.bn_stats(bn_st[:, b, :], x_sb[:, bass.ds(g * GB + b, 1), :].rearrange("p a d -> p (a d)"))
                if GB - 1 in batches:
                    i.then_inc(ln_bn, 1)

            def add_rows(gp, j, z, done):
                xx = x_sb[:, bass.ds(gp * GB + 2 * j, 2), :].rearrange("p a d -> p (a d)")
                V.tensor_tensor(xx, xx, z, ALU.add).then_inc(done, 1)

            def norm_moments():
                for b in range(GB):
                    i = V.bn_aggr(mv[:, b, :], bn_st[:, b, :])
                i.then_inc(ln_mv, 1)

            def norm_apply(n, g, T_count, batches=range(GB)):
                wait(dve, T_count[0], T_count[1])
                wait(dve, g_rstd, n + 1)
                for b in batches:
                    i = V.tensor_scalar(xn[:, b, :], x_sb[:, bass.ds(g * GB + b, 1), :].rearrange("p a d -> p (a d)"),
                                        mv[:, b, 0:1], rstd[:, b:b + 1], ALU.subtract, ALU.mult)
                if GB - 1 in batches:
                    i.then_inc(ln_xn, 1)

            dve.wait_ge(ld_x0, 16)
            norm_stats(0, 0)
            dve.wait_ge(ln_bn, 1)
            norm_moments()
            norm_apply(0, 0, (ln_T, 0))
            dve.wait_ge(g_const, 4)
            V.tensor_copy(ident_b[:, :], ident[:, :]).then_inc(idb, 1)
            def a_weights_low(part):
                for n in part:
                    what, t, kt = PREP[n]
                    dve.wait_ge(w_hi, n + 1)
                    if what == "qkv":
                        hi, lo = (w[:, kt, t * P:t * P + 512] for w in (wqkvT_hi, wqkvT_lo))
                    else:
                        hi, lo = (w[:, t:t + 2, :].rearrange("p a d -> p (a d)") for w in (wpT_hi, wpT_lo))
                    V.scalar_tensor_tensor(lo, PREP_BANKS[n][:, :], FIX * GROW if what == "qkv" else 1.0,
                                           hi.bitcast(F32), ALU.mult, ALU.subtract).then_inc(w_lo, 1)

            a_weights_low(PREP_PARTS[0])

            def xnT_low(n):
                for kt in range(KD):
                    wait(dve, ln_hi, 2 * n + kt + 1)
                    V.tensor_tensor(xnT_lo[:, kt, :], proj_ps[kt][:, :], xnT_hi[:, kt, :].bitcast(F32),
                                    ALU.subtract).then_inc(ln_lo, 1)

            def fix_blocks(g, m, dsts, scales):
                for i in range(2):
                    wait(dve, a_sgn, BLOCKS * g + m + i + 1)
                    wait(dve, a_fx, BLOCKS * g + m + i - 1)
                    V.scalar_tensor_tensor(ri[:, i, :], sgn[:, i, :], -0.5, proj_ps[i][:, :],
                                           ALU.mult, ALU.add).then_inc(a_ri, 1)
                for i in range(2):
                    wait(dve, a_ri, BLOCKS * g + m + i + 1)
                    V.tensor_scalar(dsts[i], ri[:, i, :], LOW, scales[i], ALU.max, ALU.mult).then_inc(a_fx, 1)

            def qk(g, s, n):
                wait(dve, a_S, 2 * n - 2)
                m = block_index(s)
                fix_blocks(g, m, (q_sb[:, s % 2, :], k_sb[:, s % 2, :]), (GROW / (FIX * DH ** 0.5), 1.0))

            def a_out(n):
                wait(dve, a_osgn, n + 1)
                wait(dve, a_olo, n)
                V.scalar_tensor_tensor(oi[:, :], o_sgn[:, :], -0.5, o_ps[:, :], ALU.mult, ALU.add).then_inc(a_oi, 1)
                wait(dve, a_oi, n + 1)
                wait(dve, a_pj, n)
                V.tensor_scalar(oT_hi[:, :], oi[:, :], 1.0, None, ALU.mult).then_inc(a_ohi, 1)
                wait(dve, a_ohi, n + 1)
                V.tensor_tensor(oT_lo[:, :], oi[:, :], oT_hi[:, :].bitcast(F32), ALU.subtract).then_inc(a_olo, 1)

            def a_recip(n):
                wait(dve, a_e, 2 * n + 2)
                wait(dve, a_p, n)
                V.reciprocal(rsum[:, :], sums[:, :]).then_inc(a_rs, 1)

            def y_out(g):
                wait(dve, a_pj, NP * g)
                dve.wait_ge(wb_lo, len(B_CHUNKS))
                wait(dve, a_x, 2 * g)
                bias = bias_a[:, :].rearrange("p (a d) -> p a d", a=1).broadcast_to([P, 2, D])
                for j in range(2):
                    V.tensor_tensor(raw_b[:, j * TOK:(j + 1) * TOK].rearrange("p (a d) -> p a d", a=2),
                                    y_ps[j][:, :].rearrange("p (a d) -> p a d", a=2), bias, ALU.add).then_inc(a_z, 1)

            def fix_y(g, j, part):
                z, near = raw_b[:, j * TOK:(j + 1) * TOK], near0[:, j, :]
                count = 2 * (g - 1) + j + 1
                if part == 0:
                    wait(dve, a_z, count)
                    V.tensor_scalar(near, z, 0.5, -0.5, ALU.min, ALU.max).then_inc(a_zn, 1)
                    wait(dve, a_zn, count)
                    wait(dve, a_zf, count - 1)
                    V.scalar_tensor_tensor(zi[:, :], z, GROW, near, ALU.mult, ALU.subtract).then_inc(a_zi, 1)
                else:
                    wait(dve, a_zi, count)
                    V.tensor_scalar(z, zi[:, :], LOW, 1.0 / FIX, ALU.max, ALU.mult).then_inc(a_zf, 1)

            def between_groups(g, s, first):
                if s == 1:
                    norm_stats(g + 1, (g + 1) % G)
                if s == 2:
                    norm_moments()
                if not first:
                    for slot, j, part in ((3, 0, 0), (4, 0, 1), (6, 1, 0), (7, 1, 1)):
                        if s == slot:
                            fix_y(g, j, part)
                if s in (4, 5):
                    norm_apply(g + 1, (g + 1) % G, (ln_T, 2 * g + 2), (0, 1) if s == 4 else (2, 3))

            def a_slot(g, s, first=False):
                n = NP * g + s
                base = block_index(s)
                if s == 2:
                    wait(dve, ln_bn, g + 2)
                qk(g, s, n)
                if first and s in (1, 2):
                    a_weights_low(PREP_PARTS[s + 1])
                if first and s == 1:
                    dve.wait_ge(ld_b, 16)
                    dve.wait_ge(ld_xr, 16 * (G - 1))
                    V.tensor_scalar(bias_a[:, :], bias_a[:, :], FIX, None, ALU.mult).then_inc(idb, 1)
                between_groups(g, s, first)
                if s == NP - 1:
                    xnT_low(g + 1)
                if not (first and s == 0):
                    a_recip(n - 1)
                if not (first and s < 2):
                    a_out(n - 2)
                if s < 4:
                    if s == 0 and not first:
                        wait(dve, a_av, NP * g - 4)
                    if s == 2:
                        wait(dve, a_av, NP * g)
                    fix_blocks(g, base + 2, [v_sb[:, j % 4, 512 * (j // 4):512 * (j // 4) + 512]
                                             for j in (2 * s, 2 * s + 1)], (1.0, 1.0))
                if s == 2 and not first:
                    y_out(g)
                for i in range(2):
                    wait(dve, a_ssgn, 2 * n + i + 1)
                    V.scalar_tensor_tensor(si[:, i, :], s_sgn[:, i, :], -0.5, s_ps[i][:, :], ALU.mult,
                                           ALU.add).then_inc(a_si, 1)
                for i in range(2):
                    wait(dve, a_si, 2 * n + i + 1)
                    V.tensor_scalar(si[:, i, :], si[:, i, :], LOW, None, ALU.max).then_inc(a_clip, 1)

            xnT_low(0)
            a_weights_low(PREP_PARTS[1])
            for s in range(NP):
                a_slot(0, s, first=True)
            with dve.Fori(1, G) as g:
                for s in range(NP):
                    a_slot(g, s)

            dve.wait_ge(ld_bb, 16)

            def b_v_rows(g, s, i):
                j = 2 * s + i
                wait(dve, b_blk, BLOCKS * g + block_index(s) + 2 + 2 * i)
                V.tensor_copy(v_sb[:, j % 4, 512 * (j // 4):512 * (j // 4) + 512], one_ps[:, :]).then_inc(b_v, 1)

            def b_k_rows(g, s):
                n = NP * g + s
                if isinstance(n, int) and n < 2:
                    wait(dve, a_S, 2 * (NP * G + s) - 2)
                wait(dve, b_S, 2 * n - 2)
                wait(dve, b_blk, BLOCKS * g + block_index(s) + (3 if s < 4 else 2))
                V.tensor_copy(k_sb[:, s % 2, :], one_ps[:, :]).then_inc(b_k, 1)

            def b_slot(g, s, first=False, drain=False):
                n = NP * g + s
                lag2 = not (first and s < 2) and not (drain and s >= 2)
                if not drain:
                    if s == 0:
                        wait(dve, b_chi, g + 1)
                        V.tensor_tensor(cT_lo[:, :], one_ps[:, :], cT_hi[:, :].bitcast(F32), ALU.subtract).then_inc(b_clo, 1)
                    if s == 4:
                        wait(dve, ln_bn, G + g + 2)
                if first:
                    for slot, j, part in ((3, 0, 0), (4, 0, 1), (5, 1, 0), (6, 1, 1)):
                        if s == slot:
                            fix_y(G, j, part)
                if (not (first and s == 0)) and not (drain and s >= 1):
                    for hh in range(2):
                        wait(dve, b_S, 2 * n - 1 + hh)
                        half = slice(GB * hh, GB * hh + GB)
                        V.reduce_max(mx[:, half], s_ps[hh][:, :].rearrange("p (a t) -> p a t", a=GB), AX).then_inc(b_mx, 1)
                    for hh in range(2):
                        half = slice(GB * hh, GB * hh + GB)
                        wait(dve, b_mx, 2 * n - 1 + hh)
                        V.tensor_scalar(neg_max[:, half], mx[:, half], -DH ** -0.5, None, ALU.mult).then_inc(b_nm, 1)
                if lag2:
                    wait(dve, b_T, n - 1)
                    if first and s == 2:
                        wait(dve, a_av, NP * G)
                    wait(dve, b_av, n - 2)
                    for hh in range(2):
                        i = V.tensor_copy(aT_sb[:, GB * hh:GB * hh + GB, :].rearrange("p a t -> p (a t)"),
                                          pT_ps[hh][:, :])
                    i.then_inc(b_pT, 1)
                if s == 4 and not drain:
                    norm_moments()

                if not drain:
                    av, count = (a_av, NP * G) if first else (b_av, NP * g)
                    if s == 0:
                        wait(dve, av, count - 4)
                    if s == 2:
                        wait(dve, av, count)
                    if s < 4:
                        b_v_rows(g, s, 0)
                    b_k_rows(g, s)
                if first and s == 0:
                    a_recip(NP * G - 1)
                if first and s == 2:
                    y_out(G)
                if (not (first and s == 0)) and not (drain and s >= 1):
                    wait(dve, b_e, n)
                    if first and s == 1:
                        wait(dve, a_p, NP * G)
                    wait(dve, b_p, n - 1)
                    V.reciprocal(rsum[:, :], sums[:, :]).then_inc(b_rs, 1)
                if not drain and s < 4:
                    b_v_rows(g, s, 1)
                if first and s < 2:
                    a_out(NP * G + s - 2)
                if lag2:
                    wait(dve, b_ohi, n - 1)
                    V.tensor_tensor(oT_lo[:, :], o_ps[:, :], oT_hi[:, :].bitcast(F32), ALU.subtract).then_inc(b_olo, 1)
                if s == 2 and not first:
                    wait(dve, b_pj, NP * g)
                    bias = bias_b[:, :].rearrange("p (a d) -> p a d", a=1).broadcast_to([P, 2, D])
                    for j in range(2):
                        V.tensor_tensor(near0[:, j, :].rearrange("p (a d) -> p a d", a=2),
                                        y_ps[j][:, :].rearrange("p (a d) -> p a d", a=2), bias, ALU.add).then_inc(b_z, 1)
                if not first:
                    for j in range(2):
                        if s == 4 + j and not drain:
                            wait(dve, b_z, 2 * g)
                            if j == 1:
                                wait(dve, b_x, 2 * g - 1)
                            add_rows(g - 1, j, near0[:, j, :], b_x)
                if not drain and s in (1, 3):
                    norm_stats(G + g + 1, (g + 1) % G, (0, 1) if s == 1 else (2, 3))
                if not drain and s in (5, 6):
                    norm_apply(G + g + 1, (g + 1) % G, (ln_T, 2 * (G + g) + 2), (0, 1) if s == 5 else (2, 3))
                if first and s == 7:
                    wait(dve, a_x, 2 * G + 2)
                if s == NP - 1:
                    xnT_low(G + g + 1)

            for s in range(NP):
                b_slot(0, s, first=True)
            with dve.Fori(1, G) as g:
                for s in range(NP):
                    b_slot(g, s)
            dve.wait_ge(ld_top, 16)

            def c_weights(part):
                for n in part:
                    what, t, kt = C_PREP[n]
                    dve.wait_ge(cw_hi, n + 1)
                    bank = C_BANKS[n]
                    if what == "up":
                        i = V.tensor_tensor(wiT_lo[:, kt, t * P:t * P + 512], bank[:, :],
                                            wiT_hi[:, kt, t * P:t * P + 512].bitcast(F32), ALU.subtract)
                    elif what == "down":
                        lo, hi = (w[:, t:t + 2, :].rearrange("p a d -> p (a d)") for w in (wdT_lo, wdT_hi))
                        i = V.tensor_tensor(lo, bank[:, :], hi.bitcast(F32), ALU.subtract)
                    elif what in ("lb1", "lb2"):
                        third = (lb1T if what == "lb1" else lb2T)[64:96, t * P:t * P + 512]
                        i = V.tensor_tensor(third, bank[64:96, :], third.bitcast(F32), ALU.subtract)
                    else:
                        for j in range(4):
                            i = V.tensor_tensor(laT_lo[:, :, 32 * j:32 * j + 32],
                                                bank[:, 0:64].rearrange("p (k r) -> p k r", k=KD),
                                                laT_hi[:, :, 32 * j:32 * j + 32].bitcast(F32), ALU.subtract)
                    i.then_inc(cw_lo, 1)

            for s in range(2):
                b_slot(G, s, drain=True)
                c_weights(C_PARTS[s])

            def c_slot(g, s, first=False, drain=False):
                n = NF * g + s
                if not drain:
                    if s == 3:
                        wait(dve, ln_bn, 2 * G + g + 2)
                    if s > 0:
                        c_expert0(g, s, n)
                    if s == 3:
                        norm_moments()
                if not (first and s < 2) and not (drain and s >= 2):
                    p = (s - 2) % NF
                    wait(dve, c_ghi, n - 1)
                    V.tensor_tensor(tile_lo[p % 2][:, :], hid[:, :], tile_hi[p % 2][:, :].bitcast(F32),
                                    ALU.subtract).then_inc(c_glo, 1)
                if s == NF - 1:
                    xnT_low(2 * G + g + 1)
                if not (first and s < 1) and not (drain and s >= 1):
                    p = (s - 1) % NF
                    wait(dve, c_r1, n)
                    wait(dve, c_glo, n - 1)
                    V.scalar_tensor_tensor(hid[:, :], relu1[:, :], top_sb[:, 1:2], hid0[:, p % 2, :], ALU.mult,
                                           ALU.add).then_inc(c_g, 1)
                if not drain and s == 0:
                    wait(dve, c_thi, g + 1)
                    V.tensor_tensor(lowT[32:64, :], low_ps[32:64, :], lowT[32:64, :].bitcast(F32),
                                    ALU.subtract).then_inc(c_tlo, 1)
                    if first:
                        c_weights(C_PARTS[2])
                    c_expert0(g, s, n)
                if first and s == 0:
                    b_slot(G, 2, drain=True)
                if s == 2 and not first:
                    wait(dve, c_dn, NF * g)
                    for j in range(2):
                        add_rows(g - 1, j, y_ps[j][:, :], c_x)
                if not drain and s in (0, 1):
                    norm_stats(2 * G + g + 1, (g + 1) % G, (0, 1) if s == 0 else (2, 3))
                if not drain and s in (4, 5):
                    norm_apply(2 * G + g + 1, (g + 1) % G, (ln_T, 2 * (2 * G + g) + 2), (0, 1) if s == 4 else (2, 3))
                if first and s == NF - 1:
                    wait(dve, b_x, 2 * G)

            def c_expert0(g, s, n):
                wait(dve, c_u, n + 1)
                wait(dve, c_g, n - 1)
                V.tensor_scalar(hid0[:, s % 2, :], up_ps[s % 4][:, :], 0.0, top_sb[:, 0:1], ALU.max,
                                ALU.mult).then_inc(c_g0, 1)

            for s in range(NF):
                c_slot(0, s, first=True)
            with dve.Fori(1, G) as g:
                for s in range(NF):
                    c_slot(g, s)
            for s in range(3):
                c_slot(G, s, drain=True)


INPUTS = ["x", "ctx_512", "L0_attn_w_qkv", "L0_attn_w_proj", "L0_attn_b_proj", "L0_xattn_Wq", "L0_xattn_Wk",
          "L0_xattn_Wv", "L0_xattn_Wo", "L0_xattn_bo", "L0_ffn_wi_w", "L0_ffn_wo_w", "L0_ffn_lora_As",
          "L0_ffn_lora_Bs", "L0_ffn_top_k_indices", "L0_ffn_top_k_values"]


def kernel(**inputs):
    import concourse.bacc as bacc
    from concourse.bass_utils import run_bass_kernel_spmd

    nc = bacc.Bacc("TRN2", target_bir_lowering=False, num_devices=1)
    arrays, args = {}, []
    for name in INPUTS:
        a = np.ascontiguousarray(inputs[name])
        arrays[f"in_{name}"] = a
        args.append(nc.dram_tensor(f"in_{name}", a.shape, mybir.dt.from_np(a.dtype), kind="ExternalInput").ap())
    out = nc.dram_tensor("out", (B, NT, D), F32, kind="ExternalOutput").ap()
    build(nc, *args, out)
    r = run_bass_kernel_spmd(nc, [arrays], core_ids=[0])
    return r.results[0]["out"]
```
